# Optimizing a Trainium2 kernel written in Bass

```python
import numpy as np
import jax
import jax.numpy as jnp

def _softmax(x, axis=-1):
    return jax.nn.softmax(x, axis=axis)

def _gelu(x):
    return jax.nn.gelu(x, approximate=True)

def _silu(x):
    return jax.nn.silu(x)

def _sigmoid(x):
    return jax.nn.sigmoid(x)

def _layernorm(x, axis=-1, eps=1e-05):
    m = jnp.mean(x, axis=axis, keepdims=True)
    v = jnp.var(x, axis=axis, keepdims=True)
    return (x - m) / jnp.sqrt(v + eps)

def _scatter_add(tgt, idx, src, axis=0):
    return tgt.at[idx].add(src)

def _segment_sum(src, seg, n):
    return jax.ops.segment_sum(src, seg, n)
kernel_name = 'mk_sandwich_d1_jaxref_r8_f99f95'

def setup_inputs(seed: int=0):
    np.random.seed(seed)
    _w = jnp.asarray

    def _L0_attn_setup():
        import jax, jax.numpy as jnp
        import numpy as np
        B, S, D = (4, 512, 128)
        H = 16
        K = D // H
        M = 32
        FF = 512
        EPS = 1e-06

        def _layernorm(x, g, b):
            mu = jnp.mean(x, axis=-1, keepdims=True)
            var = jnp.mean(jnp.square(x - mu), axis=-1, keepdims=True)
            return (x - mu) * jax.lax.rsqrt(var + EPS) * g + b

        def _phi(u, omega):
            proj = jnp.einsum('bhsk,mk->bhsm', u, omega)
            sq = 0.5 * jnp.sum(u * u, axis=-1, keepdims=True)
            stab = jnp.max(proj, axis=-1, keepdims=True)
            m = jnp.asarray(M, u.dtype)
            return jnp.exp(proj - sq - stab) / jnp.sqrt(m) + 1e-06

        def _performer_attn(x, wq, wk, wv, wo, omega):
            q = jnp.einsum('bsd,dhk->bhsk', x, wq)
            k = jnp.einsum('bsd,dhk->bhsk', x, wk)
            v = jnp.einsum('bsd,dhk->bhsk', x, wv)
            scale = jnp.asarray(K, x.dtype) ** (-0.25)
            pq = _phi(q * scale, omega)
            pk = _phi(k * scale, omega)
            kv = jnp.einsum('bhsm,bhsk->bhmk', pk, v)
            z = jnp.sum(pk, axis=2)
            num = jnp.einsum('bhsm,bhmk->bhsk', pq, kv)
            den = jnp.einsum('bhsm,bhm->bhs', pq, z)
            out = num / den[..., None]
            out = out.transpose(0, 2, 1, 3).reshape(x.shape[0], x.shape[1], H * K)
            return out @ wo
        key = jax.random.key(seed)
        ks = jax.random.split(key, 12)
        s_in = 1.0 / np.sqrt(D)
        s_ff = 1.0 / np.sqrt(FF)
        return {'x': jax.random.normal(ks[0], (B, S, D), jnp.float32), 'wq': jax.random.normal(ks[1], (D, H, K), jnp.float32) * s_in, 'wk': jax.random.normal(ks[2], (D, H, K), jnp.float32) * s_in, 'wv': jax.random.normal(ks[3], (D, H, K), jnp.float32) * s_in, 'wo': jax.random.normal(ks[4], (H * K, D), jnp.float32) * s_in, 'omega': jax.random.normal(ks[5], (M, K), jnp.float32), 'ln1_g': jnp.ones((D,), jnp.float32), 'ln1_b': jnp.zeros((D,), jnp.float32), 'w1': jax.random.normal(ks[6], (D, FF), jnp.float32) * s_in, 'b1': jnp.zeros((FF,), jnp.float32), 'w2': jax.random.normal(ks[7], (FF, D), jnp.float32) * s_ff, 'b2': jnp.zeros((D,), jnp.float32), 'ln2_g': jnp.ones((D,), jnp.float32), 'ln2_b': jnp.zeros((D,), jnp.float32)}
    _L0_attn_in = _L0_attn_setup()

    def _L0_ffn_setup():
        import jax, jax.numpy as jnp
        import numpy as np
        D_MODEL = 128
        N_EXPERTS = 8
        TOP_K = 2
        HIDDEN = 4 * D_MODEL
        key = jax.random.key(seed)
        ks = jax.random.split(key, 6)
        B, S = (2, 256)
        x = jax.random.normal(ks[0], (B, S, D_MODEL), dtype=jnp.float32)
        shared_w1 = jax.random.normal(ks[1], (HIDDEN, D_MODEL), dtype=jnp.float32) * 0.02
        shared_w2 = jax.random.normal(ks[2], (D_MODEL, HIDDEN), dtype=jnp.float32) * 0.02
        experts_w1 = jax.random.normal(ks[3], (N_EXPERTS, HIDDEN, D_MODEL), dtype=jnp.float32) * 0.02
        experts_w2 = jax.random.normal(ks[4], (N_EXPERTS, D_MODEL, HIDDEN), dtype=jnp.float32) * 0.02
        gate_w = jax.random.normal(ks[5], (N_EXPERTS, D_MODEL), dtype=jnp.float32) * 0.02
        return {'x': x, 'shared_w1': shared_w1, 'shared_w2': shared_w2, 'experts_w1': experts_w1, 'experts_w2': experts_w2, 'gate_w': gate_w}
    _L0_ffn_in = _L0_ffn_setup()
    _d = {'L0_attn_x': _L0_attn_in['x'], 'L0_attn_wq': _L0_attn_in['wq'], 'L0_attn_wk': _L0_attn_in['wk'], 'L0_attn_wv': _L0_attn_in['wv'], 'L0_attn_wo': _L0_attn_in['wo'], 'L0_attn_omega': _L0_attn_in['omega'], 'L0_attn_ln1_g': _L0_attn_in['ln1_g'], 'L0_attn_ln1_b': _L0_attn_in['ln1_b'], 'L0_attn_w1': _L0_attn_in['w1'], 'L0_attn_b1': _L0_attn_in['b1'], 'L0_attn_w2': _L0_attn_in['w2'], 'L0_attn_b2': _L0_attn_in['b2'], 'L0_attn_ln2_g': _L0_attn_in['ln2_g'], 'L0_attn_ln2_b': _L0_attn_in['ln2_b'], 'L0_ffn_shared_w1': _L0_ffn_in['shared_w1'], 'L0_ffn_shared_w2': _L0_ffn_in['shared_w2'], 'L0_ffn_experts_w1': _L0_ffn_in['experts_w1'], 'L0_ffn_experts_w2': _L0_ffn_in['experts_w2'], 'L0_ffn_gate_w': _L0_ffn_in['gate_w']}
    _x0 = _d['L0_attn_x']
    _d['L0_attn_x'] = jax.random.normal(jax.random.fold_in(jax.random.key(seed), 1), (2, 2048, 128), dtype=_x0.dtype)
    del _x0
    return _d

def reference(L0_attn_x, L0_attn_wq, L0_attn_wk, L0_attn_wv, L0_attn_wo, L0_attn_omega, L0_attn_ln1_g, L0_attn_ln1_b, L0_attn_w1, L0_attn_b1, L0_attn_w2, L0_attn_b2, L0_attn_ln2_g, L0_attn_ln2_b, L0_ffn_shared_w1, L0_ffn_shared_w2, L0_ffn_experts_w1, L0_ffn_experts_w2, L0_ffn_gate_w):

    def _L0_attn_ref(x, wq, wk, wv, wo, omega, ln1_g, ln1_b, w1, b1, w2, b2, ln2_g, ln2_b):
        import jax, jax.numpy as jnp
        import numpy as np
        B, S, D = (4, 512, 128)
        H = 16
        K = D // H
        M = 32
        FF = 512
        EPS = 1e-06

        def _layernorm(x, g, b):
            mu = jnp.mean(x, axis=-1, keepdims=True)
            var = jnp.mean(jnp.square(x - mu), axis=-1, keepdims=True)
            return (x - mu) * jax.lax.rsqrt(var + EPS) * g + b

        def _phi(u, omega):
            proj = jnp.einsum('bhsk,mk->bhsm', u, omega)
            sq = 0.5 * jnp.sum(u * u, axis=-1, keepdims=True)
            stab = jnp.max(proj, axis=-1, keepdims=True)
            m = jnp.asarray(M, u.dtype)
            return jnp.exp(proj - sq - stab) / jnp.sqrt(m) + 1e-06

        def _performer_attn(x, wq, wk, wv, wo, omega):
            q = jnp.einsum('bsd,dhk->bhsk', x, wq)
            k = jnp.einsum('bsd,dhk->bhsk', x, wk)
            v = jnp.einsum('bsd,dhk->bhsk', x, wv)
            scale = jnp.asarray(K, x.dtype) ** (-0.25)
            pq = _phi(q * scale, omega)
            pk = _phi(k * scale, omega)
            kv = jnp.einsum('bhsm,bhsk->bhmk', pk, v)
            z = jnp.sum(pk, axis=2)
            num = jnp.einsum('bhsm,bhmk->bhsk', pq, kv)
            den = jnp.einsum('bhsm,bhm->bhs', pq, z)
            out = num / den[..., None]
            out = out.transpose(0, 2, 1, 3).reshape(x.shape[0], x.shape[1], H * K)
            return out @ wo
        h = _performer_attn(x, wq, wk, wv, wo, omega)
        x = _layernorm(x + h, ln1_g, ln1_b)
        h2 = jax.nn.gelu(x @ w1 + b1, approximate=False) @ w2 + b2
        x = _layernorm(x + h2, ln2_g, ln2_b)
        return x

    def _L0_ffn_ref(x, shared_w1, shared_w2, experts_w1, experts_w2, gate_w):
        import jax, jax.numpy as jnp
        import numpy as np
        D_MODEL = 128
        N_EXPERTS = 8
        TOP_K = 2
        HIDDEN = 4 * D_MODEL
        B, S, D = x.shape
        T = B * S
        x_flat = x.reshape(T, D)
        shared = jnp.einsum('td,dh->th', x_flat, shared_w1.T)
        shared = jnp.einsum('th,hd->td', jax.nn.silu(shared), shared_w2.T)
        gate_logits = x_flat @ gate_w.T
        top_k_gates, top_k_idx = jax.lax.top_k(gate_logits, TOP_K)
        top_k_gates = jax.nn.softmax(top_k_gates, axis=1)
        gates = jnp.zeros((T, N_EXPERTS), dtype=x.dtype)
        gates = gates.at[jnp.arange(T)[:, None], top_k_idx].set(top_k_gates)
        h = jnp.einsum('td,ehd->teh', x_flat, experts_w1)
        expert_out = jnp.einsum('teh,edh->ted', jax.nn.silu(h), experts_w2)
        selected = jnp.einsum('ted,te->td', expert_out, gates)
        return (shared + selected).reshape(B, S, D)
    x = L0_attn_x
    x = x + _layernorm(_L0_attn_ref(_layernorm(x, axis=-1), L0_attn_wq, L0_attn_wk, L0_attn_wv, L0_attn_wo, L0_attn_omega, L0_attn_ln1_g, L0_attn_ln1_b, L0_attn_w1, L0_attn_b1, L0_attn_w2, L0_attn_b2, L0_attn_ln2_g, L0_attn_ln2_b), axis=-1)
    x = x + _layernorm(_L0_ffn_ref(_layernorm(x, axis=-1), L0_ffn_shared_w1, L0_ffn_shared_w2, L0_ffn_experts_w1, L0_ffn_experts_w2, L0_ffn_gate_w), axis=-1)
    return x

_drawn_inputs = setup_inputs


def setup_inputs(seed=0):
    import zlib

    import numpy as np

    out = dict(_drawn_inputs(seed))
    spreads = {'L0_attn_ln1_g': (1.0, 0.2),
     'L0_attn_ln1_b': (0.0, 0.1),
     'L0_attn_b1': (0.0, 0.1),
     'L0_attn_b2': (0.0, 0.1),
     'L0_attn_ln2_g': (1.0, 0.2),
     'L0_attn_ln2_b': (0.0, 0.1)}
    factors = {}
    for name, (base, spread) in spreads.items():
        noise = np.random.default_rng([zlib.crc32(name.encode()), seed]).standard_normal(out[name].shape)
        drawn = base * np.exp(spread * noise) if base else spread * noise
        out[name] = jnp.asarray(drawn.astype(out[name].dtype))
    for name, factor in factors.items():
        out[name] = (out[name] * factor).astype(out[name].dtype)
    return out
```

```python
from contextlib import ExitStack

import concourse.bass as bass
from concourse import mybir

F32 = mybir.dt.float32
F32R = mybir.dt.float32r
U32 = mybir.dt.uint32
ALU = mybir.AluOpType
ACT = mybir.ActivationFunctionType
AX_X = mybir.AxisListType.X

P = 128
D = 128
B, S = 2, 2048
T = 4
GW = T * P
GB = S // GW
NG = B * GB
NT = GB * T
H, K, M = 16, 8, 32
HM = H * M
CH = HM // P
HC = H // CH
KE = K + 1
VW = H * KE
FF = 512
FC = FF // P
E = 8
HID = 512
EC = HID // P
SCALE = float(K) ** -0.25
DELTA = 1e-6 * float(M) ** 0.5
EPS_IN, EPS_OUT = 1e-5, 1e-6
LN_EPS = [EPS_IN, EPS_OUT, EPS_OUT, EPS_IN, EPS_IN]


def build(nc, x, wqkv, wqkT, omT, wo, cols, rows, w1, w2, ew1T, ew2T, gwT, out):
    x_v = x.rearrange("b (g p t) d -> (b g) p (t d)", p=P, t=T)
    out_v = out.rearrange("b (g p t) d -> (b g) p (t d)", p=P, t=T)

    with ExitStack() as ctx:
        def sb(name, shape, dt=F32):
            return ctx.enter_context(nc.sbuf_tensor(name, shape, dt))

        def psum(name):
            return ctx.enter_context(nc.psum_tensor(name, [P, 512], F32))

        def sem(name):
            return ctx.enter_context(nc.semaphore(name))

        X = sb("X", [P, NG, GW])
        XN = sb("XN", [P, GB, GW])
        XTH = sb("XTH", [P, 2, GW], F32R)
        XTL = sb("XTL", [P, 2, GW], F32R)
        WA = H * K * 3 + 2 * HM
        W_f = sb("W_f", [P, 3 * D])
        WH = sb("WH", [P, WA], F32R)
        WL = sb("WL", [P, WA], F32R)
        wqkT_s = sb("wqkT_s", [P, 2, P])
        omT_s = sb("omT_s", [P, M])
        omBD = sb("omBD", [P, H, M])
        wo_s = sb("wo_s", [P, P])
        cols_s = sb("cols_s", [P, 2 + FC])
        rows_s = sb("rows_s", [P, 5, P])
        b12 = sb("b12", [P, P])
        w1_s = sb("w1_s", [P, FF])
        w2_s = sb("w2_s", [P, FC, P])
        gwT_s = sb("gwT_s", [P, E])
        ident = sb("ident", [P, P])
        ones = sb("ones", [P, HM])
        headmask = sb("headmask", [P, H])
        kvmask = sb("kvmask", [P, HC])
        selQ = sb("selQ", [64, HM], F32R)
        selK = sb("selK", [64, HM], F32R)
        delta = sb("delta", [P, P])
        halves = sb("halves", [P, T])
        eps = sb("eps", [P, 2, T])
        iota8 = sb("iota8", [P, E])
        iota_i = sb("iota_i", [P, E], mybir.dt.int32)
        st = sb("st", [P, 5, GB, T, 6])
        mv = sb("mv", [P, 5, GB, T, 2])
        ve = sb("ve", [P, 5, GB, T])
        rs = sb("rs", [P, 5, GB, T])
        SQ = sb("SQ", [P, 2, 2 * D])
        VX = sb("VX", [P, 3, H, KE])
        MX = sb("MX", [P, NT, 2, H])
        SS = sb("SS", [P, NT, 2, H])
        CC = sb("CC", [P, NT, 2, H])
        CHL = sb("CHL", [P, 2, 4, 2, H], F32R)
        held = sb("held", [P, 1])
        CT = sb("CT", [64, 2, GW], F32R)
        PK = sb("PK", [P, 2, HM])
        KVB = sb("KVB", [P, VW])
        DS = sb("DS", [P, VW])
        NB = sb("NB", [P, 2, 2, H, KE])
        RD = sb("RD", [P, 2, 2, H])
        AT = sb("AT", [P, T, H, K])
        ATT = sb("ATT", [P, GW])
        R1 = sb("R1", [P, 2, GW])
        N1 = sb("N1", [P, 2, GW])
        X2 = sb("X2", [P, 2, GW])
        X1T = sb("X1T", [P, GW])
        HT = sb("HT", [P, FC, GW])
        XFT = sb("XFT", [P, GW])
        XFH = sb("XFH", [P, NG, GW], F32R)
        XFL = sb("XFL", [P, NG, GW], F32R)
        LG = sb("LG", [P, T, E])
        V8 = sb("V8", [P, T, 8])
        I8 = sb("I8", [P, T, 8], U32)
        I8f = sb("I8f", [P, T, 2])
        GA = sb("GA", [P, T])
        GT = sb("GT", [P, T, 2])
        OH = sb("OH", [P, 2, T, E])
        GATE = sb("GATE", [P, NG, T, E])
        E2 = sb("E2", [P, (E + 1) * EC, P])
        st5 = sb("st5", [P, T, 6])
        mv5 = sb("mv5", [P, T, 2])
        ve5 = sb("ve5", [P, T])
        rs5 = sb("rs5", [P, T])

        sel_f = X2[0:64]
        sel_ab = [R1[0:64, i, :] for i in range(2)] + [N1[0:64, i, :] for i in range(2)]
        ST1 = X2
        HS = HT
        ACC, n5, OUT = X1T, XFT, ATT
        with nc.sbuf_tensor("PQT", [P, GB, CH, GW], F32) as PQT:
            pass
        E1H = sb("E1H", [P, (E + 1) * HID], F32R)
        E1L = sb("E1L", [P, (E + 1) * HID], F32R)

        pT, pQKV, pPQ = psum("pT"), psum("pQKV"), psum("pPQ")
        pPK = [psum("pPK0"), psum("pPK1")]
        pF = [psum("pF0"), psum("pF1")]
        pKV = psum("pKV")

        s_x = [sem(f"x_loaded{g}") for g in range(GB)]
        s_w = sem("weights_loaded")
        s_w2 = sem("expert_w2_loaded")
        s_stage = [sem(f"staged{i}") for i in range(2)]
        s_split = sem("expert_w1_split")
        s_split_h = sem("expert_w1_hi")
        s_const = sem("constants_by_pool")
        s_prep_p = sem("prep_products")
        s_prep_v = sem("prep_by_dve")
        s_batch = sem("batch_done")
        s_bn = [sem(f"bn_stats{j}") for j in range(5)]
        s_mv = [sem(f"mean_var{j}") for j in range(5)]
        s_ve = [sem(f"var_eps{j}") for j in range(5)]
        s_rs = [sem(f"rstd{j}") for j in range(5)]
        s_no = [sem(f"normed{j}") for j in range(5)]
        s_xT, s_xh, s_xl = sem("xn_turned"), sem("xn_hi"), sem("xn_lo")
        s_qkv, s_pk, s_pq = sem("qkv_ready"), sem("pk_raw"), sem("pq_raw")
        s_sq, s_vx = sem("squares"), sem("v_copied")
        s_mxk, s_mxq, s_ss, s_cc, s_ch, s_cl = (sem(n) for n in ("max_k", "max_q", "sq_sum", "c_sum", "c_hi", "c_lo"))
        s_cT, s_ct, s_pkb, s_ek = sem("c_turned"), sem("c_copied"), sem("pk_biased"), sem("exp_k")
        s_kv, s_kvall = sem("kv_step"), sem("kv_masked")
        s_fm, s_eq = sem("pq_biased"), sem("exp_q")
        s_ds, s_dsc = sem("dsum"), sem("dsum_copied")
        s_num, s_nb, s_rd, s_at = sem("num_den"), sem("num_den_copied"), sem("den_recip"), sem("attn")
        s_aT, s_att, s_wo, s_r1 = sem("attn_turned"), sem("attn_copied"), sem("wo_done"), sem("res1")
        s_n1g, s_x2 = sem("n1_times_g"), sem("x2_ready")
        s_nT, s_x1t, s_up, s_ge, s_dn, s_r2 = (sem(n) for n in ("n1_turned", "x1t", "up_done", "gelu_done", "down_done", "res2"))
        s_n2g, s_y, s_x1 = sem("n2_times_g"), sem("y_ready"), sem("x1_ready")
        s_fT, s_xft, s_xfh, s_xfl, s_lg, s_lgc = (sem(n) for n in ("xf_turned", "xf_copied", "xf_hi", "xf_lo", "logits", "logits_copied"))
        s_v8, s_i8, s_if, s_gd, s_th, s_gt, s_oh, s_gate = (sem(n) for n in (
            "top8", "top8_index", "index_float", "top2_gap", "tanh_gap", "top2_gates", "onehots", "gates"))
        s_u, s_si, s_do, s_acc = sem("exp_up"), sem("silu_done"), sem("exp_down"), sem("acc")
        s_bn5, s_mv5, s_ve5, s_rs5, s_no5, s_out, s_st = (sem(n) for n in (
            "bn5", "mv5", "ve5", "rs5", "no5", "out_ready", "stored"))

        NLOADS = 9

        def group(v, *idx):
            return v[(slice(None), *idx)]

        block = ctx.enter_context(nc.Block())

        @block.sync
        def _(sp):
            sp.dma_start(X[:, 0, :], x_v[0]).then_inc(s_x[0], 16)
            sp.dma_start(W_f[:], wqkv).then_inc(s_w, 16)
            sp.dma_start(wqkT_s[:], wqkT).then_inc(s_w, 16)
            sp.dma_start(omT_s[:], omT).then_inc(s_w, 16)
            for g in range(1, GB):
                sp.dma_start(X[:, g, :], x_v[g]).then_inc(s_x[g], 16)
            sp.dma_start(wo_s[:], wo).then_inc(s_w, 16)
            sp.dma_start(cols_s[:], cols).then_inc(s_w, 16)
            sp.dma_start(rows_s[:].rearrange("p v d -> p (v d)"), rows.to_broadcast([P, 5 * P])).then_inc(s_w, 16)
            sp.dma_start(w1_s[:], w1).then_inc(s_w, 16)
            sp.dma_start(w2_s[:], w2).then_inc(s_w, 16)
            sp.dma_start(gwT_s[:], gwT).then_inc(s_w, 16)
            for g in range(GB):
                sp.wait_ge(s_x[g], 16)
                sp.dma_start(X[:, GB + g, :], x_v[GB + g]).then_inc(s_x[g], 16)
            sp.wait_ge(s_batch, B + 1)
            for e in range(E + 1):
                if e >= 2:
                    sp.wait_ge(s_split, e - 1)
                sp.dma_start(ST1[:, e % 2, :], ew1T[e]).then_inc(s_stage[e % 2], 16)
            sp.dma_start(E2[:], ew2T).then_inc(s_w2, 16)
            with sp.Fori(0, NG) as n:
                sp.wait_ge(s_out, n + 1)
                sp.dma_start(out_v[bass.ds(n, 1)].rearrange("n p f -> (n p) f"), OUT[:]).then_inc(s_st, 16)
            sp.wait_ge(s_st, 16 * NG + 16)

        @block.gpsimd
        def _(pool):
            eng = nc.gpsimd
            eng.memset(ones[:], 1.0).then_inc(s_const, 1)
            eng.memset(delta[:], DELTA).then_inc(s_const, 1)
            eng.memset(eps[:, 0, :], EPS_IN)
            eng.memset(eps[:, 1, :], EPS_OUT)
            eng.memset(halves[:], -0.5).then_inc(s_const, 1)
            eng.memset(sel_f[:], -1.0).then_inc(s_const, 1)
            eng.memset(VX[:], 1.0).then_inc(s_const, 1)
            eng.iota(iota_i[:], pattern=[[1, E]], base=0, channel_multiplier=0).then_inc(s_const, 1)
            pool.wait_ge(s_const, 6)
            eng.tensor_copy(iota8[:], iota_i[:]).then_inc(s_const, 1)
            eng.affine_select(out=ident[:], in_=ones[:, 0:P], compare_op=ALU.is_equal, fill=0.0, base=0,
                              pattern=[[-1, P]], channel_multiplier=1).then_inc(s_const, 1)
            eng.affine_select(out=headmask[:], in_=ones[:, 0:H], compare_op=ALU.is_ge, fill=0.0, base=0,
                              pattern=[[-K, H]], channel_multiplier=1).then_inc(s_const, 1)
            eng.affine_select(out=kvmask[:], in_=ones[:, 0:HC], compare_op=ALU.is_ge, fill=0.0, base=0,
                              pattern=[[-M, HC]], channel_multiplier=1).then_inc(s_const, 1)
            pool.wait_ge(s_const, 10)
            eng.affine_select(out=headmask[:], in_=headmask[:], compare_op=ALU.is_ge, fill=0.0, base=K - 1,
                              pattern=[[K, H]], channel_multiplier=-1).then_inc(s_const, 1)
            eng.affine_select(out=kvmask[:], in_=kvmask[:], compare_op=ALU.is_ge, fill=0.0, base=M - 1,
                              pattern=[[M, HC]], channel_multiplier=-1).then_inc(s_const, 1)
            sel = [sel_f[:, i, :].rearrange("p (h m) -> p h m", m=M) for i in range(2)]
            done = 12
            for i in range(2):
                lo, hi = 2 * H * i, 2 * H * i + H
                ab = sel_ab[2 * i:2 * i + 2]
                for a, off in enumerate((lo, hi)):
                    eng.affine_select(out=ab[a].rearrange("p (h m) -> p h m", m=M), in_=sel[i],
                                      compare_op=ALU.is_equal, fill=0.0, base=-off,
                                      pattern=[[-1, H], [0, M]], channel_multiplier=1).then_inc(s_const, 1)
                done += 2
                pool.wait_ge(s_const, done)
                eng.tensor_tensor(sel_f[:, i, :], ab[0], ab[1], ALU.add).then_inc(s_const, 1)
                done += 1
            pool.wait_ge(s_w, 16 * NLOADS)
            eng.tensor_tensor(b12[:], rows_s[:, 1, :], rows_s[:, 2, :], ALU.add).then_inc(s_const, 1)

            def rstd(b, j, g):
                pool.wait_ge(s_mv[j], b * GB + g + 1)
                eng.tensor_tensor(ve[:, j, g, :], mv[:, j, g, :, 1], eps[:, int(LN_EPS[j] == EPS_OUT), :], ALU.add).then_inc(s_ve[j], 1)
                pool.wait_ge(s_ve[j], b * GB + g + 1)
                eng.tensor_tensor(rs[:, j, g, :], ve[:, j, g, :], halves[:], ALU.pow).then_inc(s_rs[j], 1)

            def affine(b, j, g, dst, gain, bias, s_mid, s_end):
                pool.wait_ge(s_no[j], b * GB + g + 1)
                v = dst.rearrange("p (t d) -> p t d", t=T)
                n = N1[:, g % 2, :].rearrange("p (t d) -> p t d", t=T)
                eng.tensor_tensor(v, n, gain.unsqueeze(1).to_broadcast([P, T, D]), ALU.mult).then_inc(s_mid, 1)
                pool.wait_ge(s_mid, b * GB + g + 1)
                eng.tensor_tensor(v, v, bias.unsqueeze(1).to_broadcast([P, T, D]), ALU.add).then_inc(s_end, 1)

            with pool.Fori(0, B) as b:
                pool.wait_ge(s_batch, b + 1)
                for g in range(GB):
                    rstd(b, 0, g)
                for g in range(GB):
                    rstd(b, 1, g)
                    affine(b, 1, g, X2[:, g % 2, :], rows_s[:, 0, :], b12[:], s_n1g, s_x2)
                    rstd(b, 2, g)
                    affine(b, 2, g, R1[:, g % 2, :], rows_s[:, 3, :], rows_s[:, 4, :], s_n2g, s_y)
                    rstd(b, 3, g)
                    pool.wait_ge(s_no[3], b * GB + g + 1)
                    xg = X[:, bass.ds(b * GB + g, 1), :].rearrange("p n f -> p (n f)")
                    eng.tensor_tensor(xg, xg, N1[:, g % 2, :], ALU.add).then_inc(s_x1, 1)
                    rstd(b, 4, g)
            with pool.Fori(0, NG) as n:
                pool.wait_ge(s_mv5, n + 1)
                eng.tensor_tensor(ve5[:], mv5[:, :, 1], eps[:, 0, :], ALU.add).then_inc(s_ve5, 1)
                pool.wait_ge(s_ve5, n + 1)
                eng.tensor_tensor(rs5[:], ve5[:], halves[:], ALU.pow).then_inc(s_rs5, 1)

        @block.tensor
        def _(pe):
            def three(o, a, b_, start=True, stop=True):
                nc.tensor.matmul(o, a[0], b_[0], start=start, stop=False)
                nc.tensor.matmul(o, a[0], b_[1], start=False, stop=False)
                return nc.tensor.matmul(o, a[1], b_[0], start=False, stop=stop)

            pe.wait_ge(s_prep_v, 2)
            for i in range(2):
                nc.tensor.matmul(pF[i][:], wqkT_s[:, i, :], omBD[:].rearrange("p h m -> p (h m)"),
                                 start=True, stop=True).then_inc(s_prep_p, 1)
            pe.wait_ge(s_prep_v, 11)

            def turn_xn(b, g):
                pe.wait_ge(s_no[0], b * GB + g + 1)
                for t in range(T):
                    m = nc.tensor.transpose(pT[:, t * P:(t + 1) * P], XN[:, g, t * P:(t + 1) * P], ident[:])
                m.then_inc(s_xT, 1)

            def tile_products(b, i):
                g, t = i // T, i % T
                if t == 0:
                    pe.wait_ge(s_xl, b * GB + g + 1)
                xt = [v[:, g % 2, t * P:(t + 1) * P] for v in (XTH, XTL)]
                w = lambda a, n: [v[:, a:a + n] for v in (WH, WL)]
                if i:
                    pe.wait_ge(s_vx, b * NT + i)
                three(pQKV[:, 0:3 * D], xt, w(0, 3 * D)).then_inc(s_qkv, 1)
                if i >= 2:
                    pe.wait_ge(s_ek, b * NT + i - 1)
                three(pPK[i % 2][:], xt, w(3 * D + HM, HM)).then_inc(s_pk, 1)
                if i:
                    pe.wait_ge(s_mxq, b * NT + i)
                three(pPQ[:], xt, w(3 * D, HM)).then_inc(s_pq, 1)

            def bias_k(b, i):
                g, t = i // T, i % T
                pe.wait_ge(s_cl, b * NT + i + 1)
                if t == 2 and g + 1 < GB:
                    pe.wait_ge(s_xl, b * GB + g + 2)
                nc.tensor.transpose(pT[:, 0:P], CHL[:, i % 2].rearrange("p a c h -> p (a c h)").bitcast(F32),
                                    ident[:]).then_inc(s_cT, 1)
                pe.wait_ge(s_ct, b * NT + i + 1)
                pe.wait_ge(s_mxk, b * NT + i + 1)
                nc.tensor.matmul(pPK[i % 2][:], CT[:, g % 2, t * P:(t + 1) * P], selK[:],
                                 start=False, stop=True, skip_group_check=True).then_inc(s_pkb, 1)

            def sum_kv(b, i):
                pe.wait_ge(s_ek, b * NT + i + 1)
                pe.wait_ge(s_vx, b * NT + i + 1)
                v = VX[:, i % 3].rearrange("p h k -> p (h k)")
                nc.tensor.matmul(pKV[:, 0:VW], delta[:], v, start=(i == 0), stop=False, skip_group_check=True)
                for c in range(CH):
                    w = HC * KE
                    m = nc.tensor.matmul(pKV[:, c * w:(c + 1) * w], PK[:, i % 2, c * P:(c + 1) * P],
                                         v[:, c * w:(c + 1) * w], start=False, stop=(i == NT - 1 and c == CH - 1),
                                         skip_group_check=True)
                m.then_inc(s_kv, 1)

            def features_q(b, g):
                xt = [v[:, g % 2, :] for v in (XTH, XTL)]
                for c in range(CH):
                    if g * CH + c >= 2:
                        pe.wait_ge(s_eq, b * GB * CH + g * CH + c - 1)
                    w = [v[:, 3 * D + c * P:3 * D + (c + 1) * P] for v in (WH, WL)]
                    three(pF[c % 2][:], w, xt, stop=False)
                    nc.tensor.matmul(pF[c % 2][:], selQ[:, c * P:(c + 1) * P], CT[:, g % 2, :],
                                     start=False, stop=True).then_inc(s_fm, 1)

            def attend(b, g):
                if g:
                    pe.wait_ge(s_nb, b * 2 * GB + 2 * g)
                w = HC * KE
                for t in range(T):
                    for c in range(CH):
                        a = (t % 2) * VW + c * w
                        m = nc.tensor.matmul(pF[t // 2][:, a:a + w], PQT[:, g, c, t * P:(t + 1) * P],
                                             KVB[:, c * w:(c + 1) * w], start=True, stop=True)
                    if t % 2:
                        m.then_inc(s_num, 1)
                pe.wait_ge(s_at, b * 2 * GB + 2 * g + 2)
                for t in range(T):
                    m = nc.tensor.transpose(pT[:, t * P:(t + 1) * P], AT[:, t].rearrange("p h k -> p (h k)"), ident[:])
                m.then_inc(s_aT, 1)
                pe.wait_ge(s_att, b * GB + g + 1)
                if g:
                    pe.wait_ge(s_r1, b * GB + g)
                for t in range(T):
                    m = nc.tensor.matmul(pPQ[:, t * P:(t + 1) * P], ATT[:, t * P:(t + 1) * P], wo_s[:],
                                         start=True, stop=True)
                m.then_inc(s_wo, 1)

            def mlp(b, g):
                pe.wait_ge(s_no[1], b * GB + g + 1)
                for t in range(T):
                    m = nc.tensor.transpose(pT[:, t * P:(t + 1) * P], N1[:, g % 2, t * P:(t + 1) * P], ident[:])
                m.then_inc(s_nT, 1)
                pe.wait_ge(s_x1t, b * GB + g + 1)
                for c in range(FC):
                    if g * FC + c >= 2:
                        pe.wait_ge(s_ge, b * GB * FC + g * FC + c - 1)
                    nc.tensor.matmul(pPK[c % 2][:], w1_s[:, c * P:(c + 1) * P], X1T[:],
                                     start=True, stop=True).then_inc(s_up, 1)
                pe.wait_ge(s_ge, b * GB * FC + (g + 1) * FC)
                if g:
                    pe.wait_ge(s_r2, b * GB + g)
                for t in range(T):
                    for c in range(FC):
                        m = nc.tensor.matmul(pQKV[:, t * P:(t + 1) * P], HT[:, c, t * P:(t + 1) * P], w2_s[:, c, :],
                                             start=(c == 0), stop=(c == FC - 1))
                m.then_inc(s_dn, 1)

            def gate_products(b, g):
                pe.wait_ge(s_no[4], b * GB + g + 1)
                for t in range(T):
                    m = nc.tensor.transpose(pT[:, t * P:(t + 1) * P], N1[:, g % 2, t * P:(t + 1) * P], ident[:])
                m.then_inc(s_fT, 1)
                pe.wait_ge(s_xfl, b * GB + g + 1)
                for t in range(T):
                    m = nc.tensor.matmul(pT[:, t * E:(t + 1) * E], XFT[:, t * P:(t + 1) * P], gwT_s[:],
                                         start=True, stop=True)
                m.then_inc(s_lg, 1)
                pe.wait_ge(s_lgc, b * GB + g + 1)

            with pe.Fori(0, B) as b:
                pe.wait_ge(s_batch, b + 1)
                turn_xn(b, 0)
                for i in range(NT + 2):
                    if i < NT:
                        tile_products(b, i)
                    if 1 <= i <= NT:
                        bias_k(b, i - 1)
                    if i >= 2:
                        sum_kv(b, i - 2)
                    if i % T == 1 and i > 1:
                        features_q(b, i // T - 1)
                    if i % T == 2 and i < NT - T:
                        turn_xn(b, i // T + 1)
                pe.wait_ge(s_kvall, b + 1)
                nc.tensor.matmul(pT[:, 0:VW], delta[:], KVB[:], start=True, stop=True).then_inc(s_ds, 1)
                pe.wait_ge(s_dsc, b + 1)
                pe.wait_ge(s_eq, (b + 1) * GB * CH)
                for g in range(GB):
                    attend(b, g)
                    mlp(b, g)
                    gate_products(b, g)

            pe.wait_ge(s_batch, B + 1)
            pe.wait_ge(s_split, E + 1)
            pe.wait_ge(s_w2, 16)
            with pe.Fori(0, NG) as n:
                NC = (E + 1) * EC
                banks = [pF[0], pF[1], pPK[0], pPK[1]]
                xf = [v[:, bass.ds(n, 1), :].rearrange("p n f -> p (n f)") for v in (XFH, XFL)]

                def up(k):
                    pe.wait_ge(s_si, n * NC + k + 1)
                    w = [v[:, k * P:(k + 1) * P] for v in (E1H, E1L)]
                    three(banks[k % 4][:], w, xf).then_inc(s_u, 1)

                up(0)
                up(1)
                for k in range(NC):
                    e, c = k // EC, k % EC
                    o = (pQKV, pPQ)[e % 2]
                    if k + 2 < NC:
                        up(k + 2)
                    pe.wait_ge(s_si, n * NC + k + 5)
                    if c == 0:
                        pe.wait_ge(s_acc, n * (E + 1) + max(e, 1) + 1)
                    for t in range(T):
                        m = nc.tensor.matmul(o[:, t * P:(t + 1) * P], HS[:, k % 4, t * P:(t + 1) * P], E2[:, k, :],
                                             start=(c == 0 and t == 0), stop=(c == EC - 1), skip_group_check=True)
                    m.then_inc(s_do, 1)

        @block.scalar
        def _(act):
            A = nc.scalar.activation

            def squares(b, i):
                act.wait_ge(s_qkv, b * NT + i + 1)
                if i >= 2:
                    act.wait_ge(s_ss, b * NT + i - 1)
                A(SQ[:, i % 2, :], pQKV[:, 0:2 * D], ACT.Square, scale=SCALE * 0.5 ** 0.5).then_inc(s_sq, 1)
                if i >= 3:
                    act.wait_ge(s_kv, b * NT + i - 2)
                A(VX[:, i % 3, :, 0:K], pQKV[:, 2 * D:3 * D].rearrange("p (h k) -> p h k", k=K),
                  ACT.Copy).then_inc(s_vx, 1)

            def exp_k(b, i):
                g, t = i // T, i % T
                act.wait_ge(s_cT, b * NT + i + 1)
                A(CT[:, g % 2, t * P:(t + 1) * P], pT[0:64, 0:P], ACT.Copy).then_inc(s_ct, 1)
                act.wait_ge(s_pkb, b * NT + i + 1)
                if i >= 2:
                    act.wait_ge(s_kv, b * NT + i - 1)
                A(PK[:, i % 2, :], pPK[i % 2][:], ACT.Exp).then_inc(s_ek, 1)

            def exp_q(b, g):
                for c in range(CH):
                    act.wait_ge(s_fm, (b * GB + g) * CH + c + 1)
                    A(PQT[:, g, c, :], pF[c % 2][:], ACT.Exp).then_inc(s_eq, 1)

            def hi_xn(b, g):
                act.wait_ge(s_xT, b * GB + g + 1)
                A(XTH[:, g % 2, :], pT[:], ACT.Copy).then_inc(s_xh, 1)

            act.wait_ge(s_const, 5)
            with act.Fori(0, B) as b:
                act.wait_ge(s_batch, b + 1)
                hi_xn(b, 0)
                for i in range(NT + 2):
                    if i < NT:
                        squares(b, i)
                    if 1 <= i <= NT:
                        exp_k(b, i - 1)
                    if i % T == 1 and i > 1:
                        exp_q(b, i // T - 1)
                    if i % T == 2 and i < NT - T:
                        hi_xn(b, i // T + 1)
                for g in range(GB):
                    act.wait_ge(s_aT, b * GB + g + 1)
                    if g:
                        act.wait_ge(s_wo, b * GB + g)
                    A(ATT[:], pT[:], ACT.Copy).then_inc(s_att, 1)
                    act.wait_ge(s_nT, b * GB + g + 1)
                    A(X1T[:], pT[:], ACT.Identity, scale=cols_s[:, 0:1], bias=cols_s[:, 1:2]).then_inc(s_x1t, 1)
                    for c in range(FC):
                        act.wait_ge(s_up, (b * GB + g) * FC + c + 1)
                        A(HT[:, c, :], pPK[c % 2][:], ACT.Gelu, bias=cols_s[:, 2 + c:3 + c]).then_inc(s_ge, 1)
                    n = b * GB + g
                    act.wait_ge(s_fT, n + 1)
                    A(XFT[:], pT[:], ACT.Copy).then_inc(s_xft, 1)
                    A(XFH[:, bass.ds(n, 1), :].rearrange("p n f -> p (n f)"), pT[:], ACT.Copy).then_inc(s_xfh, 1)
                    act.wait_ge(s_gd, n + 1)
                    A(GT[:, :, 0], GA[:], ACT.Tanh, scale=0.5).then_inc(s_th, 1)
            act.wait_ge(s_ge, B * GB * FC)
            nc.scalar.sem_inc(s_si, 4)
            with act.Fori(0, NG) as n:
                NC = (E + 1) * EC
                banks = [pF[0], pF[1], pPK[0], pPK[1]]
                for k in range(NC):
                    act.wait_ge(s_u, n * NC + k + 1)
                    act.wait_ge(s_do, n * NC + k + 1)
                    A(HS[:, k % 4, :], banks[k % 4][:], ACT.Silu).then_inc(s_si, 1)

        @block.vector
        def _(dve):
            v = nc.vector

            dve.wait_ge(s_w, 16 * NLOADS)
            dve.wait_ge(s_const, 19)
            v.tensor_tensor(omBD[:], omT_s[:].unsqueeze(1).to_broadcast([P, H, M]),
                            headmask[:].unsqueeze(2).to_broadcast([P, H, M]), ALU.mult).then_inc(s_prep_v, 1)
            dve.wait_ge(s_prep_v, 1)
            v.tensor_scalar(omBD[:], omBD[:], SCALE, None, ALU.mult).then_inc(s_prep_v, 1)
            v.tensor_copy(WH[:, 0:3 * D], W_f[:]).then_inc(s_prep_v, 1)
            v.tensor_copy(selQ[:], sel_f[:, 0, :]).then_inc(s_prep_v, 1)
            v.tensor_copy(selK[:], sel_f[:, 1, :]).then_inc(s_prep_v, 1)
            dve.wait_ge(s_prep_v, 3)
            v.tensor_tensor(WL[:, 0:3 * D], W_f[:], WH[:, 0:3 * D].bitcast(F32), ALU.subtract).then_inc(s_prep_v, 1)
            n = 6
            for i in range(2):
                a = slice(3 * D + i * HM, 3 * D + (i + 1) * HM)
                dve.wait_ge(s_prep_p, i + 1)
                v.tensor_copy(WH[:, a], pF[i][:]).then_inc(s_prep_v, 1)
                n += 1
                dve.wait_ge(s_prep_v, n)
                v.tensor_tensor(WL[:, a], pF[i][:], WH[:, a].bitcast(F32), ALU.subtract).then_inc(s_prep_v, 1)
                n += 1
            v.memset(CHL[:, :, 2:4].bitcast(F32), 0.0).then_inc(s_prep_v, 1)
            dve.wait_ge(s_prep_v, 11)

            def hold(s, value):
                dve.wait_ge(s, value)
                v.memset(held[:], 0.0)

            def stats(b, j, g, src):
                for t in range(T):
                    s = v.bn_stats(st[:, j, g, t, :], src[:, t * D:(t + 1) * D])
                s.then_inc(s_bn[j], 1)
                hold(s_bn[j], b * GB + g + 1)
                for t in range(T):
                    s = v.bn_aggr(mv[:, j, g, t, :], st[:, j, g, t, :])
                s.then_inc(s_mv[j], 1)

            def norm(b, j, g, dst, src):
                dve.wait_ge(s_rs[j], b * GB + g + 1)
                for t in range(T):
                    s = v.tensor_scalar(dst[:, t * D:(t + 1) * D], src[:, t * D:(t + 1) * D],
                                        mv[:, j, g, t, 0:1], rs[:, j, g, t:t + 1], ALU.subtract, ALU.mult)
                s.then_inc(s_no[j], 1)

            def lo_xn(b, g):
                dve.wait_ge(s_xh, b * GB + g + 1)
                v.tensor_tensor(XTL[:, g % 2, :], pT[:], XTH[:, g % 2, :].bitcast(F32),
                                ALU.subtract).then_inc(s_xl, 1)

            def xg(b, g):
                return X[:, bass.ds(b * GB + g, 1), :].rearrange("p n f -> p (n f)")

            def bias_parts(b, i):
                k = b * NT + i + 1
                dve.wait_ge(s_pk, k)
                v.tensor_reduce(MX[:, i, 1, :], pPK[i % 2][:].rearrange("p (h m) -> p h m", m=M), AX_X,
                                ALU.max).then_inc(s_mxk, 1)
                dve.wait_ge(s_pq, k)
                v.tensor_reduce(MX[:, i, 0, :], pPQ[:].rearrange("p (h m) -> p h m", m=M), AX_X,
                                ALU.max).then_inc(s_mxq, 1)
                dve.wait_ge(s_sq, k)
                v.tensor_reduce(SS[:, i], SQ[:, i % 2, :].rearrange("p (a h k) -> p a h k", a=2, k=K), AX_X,
                                ALU.add).then_inc(s_ss, 1)
                dve.wait_ge(s_ss, k)
                dve.wait_ge(s_mxq, k)
                v.tensor_tensor(CC[:, i], MX[:, i], SS[:, i], ALU.add).then_inc(s_cc, 1)
                dve.wait_ge(s_cc, k)
                if i >= 2:
                    dve.wait_ge(s_cT, k - 2)
                v.tensor_copy(CHL[:, i % 2, 0:2, 0, :], CC[:, i]).then_inc(s_ch, 1)
                dve.wait_ge(s_ch, k)
                v.tensor_tensor(CHL[:, i % 2, 0:2, 1, :], CC[:, i], CHL[:, i % 2, 0:2, 0, :].bitcast(F32),
                                ALU.subtract).then_inc(s_cl, 1)

            nc.vector.sem_inc(s_batch, 1)
            with dve.Fori(0, B) as b:
                dve.wait_ge(s_batch, b + 1)
                dve.wait_ge(s_x[0], b * 16 + 16)
                stats(b, 0, 0, xg(b, 0))
                norm(b, 0, 0, XN[:, 0], xg(b, 0))
                lo_xn(b, 0)
                for i in range(NT):
                    g = i // T
                    bias_parts(b, i)
                    if g + 1 < GB:
                        if i % T == 0:
                            dve.wait_ge(s_x[g + 1], b * 16 + 16)
                            stats(b, 0, g + 1, xg(b, g + 1))
                        if i % T == 1:
                            norm(b, 0, g + 1, XN[:, g + 1], xg(b, g + 1))
                        if i % T == 2:
                            lo_xn(b, g + 1)
                dve.wait_ge(s_kv, (b + 1) * NT)
                v.tensor_tensor(KVB[:].rearrange("p (c j k) -> p c j k", c=CH, j=HC),
                                pKV[:, 0:VW].rearrange("p (c j k) -> p c j k", c=CH, j=HC),
                                kvmask[:].unsqueeze(1).unsqueeze(3).to_broadcast([P, CH, HC, KE]),
                                ALU.mult).then_inc(s_kvall, 1)
                dve.wait_ge(s_ds, b + 1)
                v.tensor_copy(DS[:], pT[:, 0:VW]).then_inc(s_dsc, 1)
                dve.wait_ge(s_dsc, b + 1)
                for g in range(GB):
                    n = b * GB + g
                    for h in range(2):
                        k = 2 * n + h + 1
                        dve.wait_ge(s_num, k)
                        nb = NB[:, h].rearrange("p t h k -> p t (h k)")
                        v.tensor_tensor(nb, pF[h][:, 0:2 * VW].rearrange("p (t w) -> p t w", t=2),
                                        DS[:].unsqueeze(1).to_broadcast([P, 2, VW]), ALU.add).then_inc(s_nb, 1)
                        dve.wait_ge(s_nb, k)
                        v.reciprocal(RD[:, h], NB[:, h, :, :, K]).then_inc(s_rd, 1)
                        dve.wait_ge(s_rd, k)
                        v.tensor_tensor(AT[:, 2 * h:2 * h + 2], NB[:, h, :, :, 0:K],
                                        RD[:, h].unsqueeze(3).to_broadcast([P, 2, H, K]), ALU.mult).then_inc(s_at, 1)
                    r, nn = R1[:, g % 2, :], N1[:, g % 2, :]
                    dve.wait_ge(s_wo, n + 1)
                    v.tensor_tensor(r, pPQ[:], XN[:, g], ALU.add).then_inc(s_r1, 1)
                    dve.wait_ge(s_r1, n + 1)
                    stats(b, 1, g, r)
                    norm(b, 1, g, nn, r)
                    dve.wait_ge(s_x2, n + 1)
                    dve.wait_ge(s_dn, n + 1)
                    v.tensor_tensor(r, pQKV[:], X2[:, g % 2, :], ALU.add).then_inc(s_r2, 1)
                    dve.wait_ge(s_r2, n + 1)
                    stats(b, 2, g, r)
                    norm(b, 2, g, nn, r)
                    dve.wait_ge(s_y, n + 1)
                    stats(b, 3, g, r)
                    norm(b, 3, g, nn, r)
                    hold(s_x1, n + 1)
                    stats(b, 4, g, xg(b, g))
                    norm(b, 4, g, nn, xg(b, g))
                    dve.wait_ge(s_xfh, n + 1)
                    v.tensor_tensor(XFL[:, bass.ds(n, 1), :].rearrange("p n f -> p (n f)"), pT[:],
                                    XFH[:, bass.ds(n, 1), :].rearrange("p n f -> p (n f)").bitcast(F32),
                                    ALU.subtract).then_inc(s_xfl, 1)
                    dve.wait_ge(s_lg, n + 1)
                    v.tensor_copy(LG[:].rearrange("p t e -> p (t e)"), pT[:, 0:T * E]).then_inc(s_lgc, 1)
                    hold(s_lgc, n + 1)
                    for t in range(T):
                        s = v.max(V8[:, t, :], LG[:, t, :])
                    s.then_inc(s_v8, 1)
                    hold(s_v8, n + 1)
                    for t in range(T):
                        s = v.max_index(I8[:, t, :], V8[:, t, :], LG[:, t, :])
                    s.then_inc(s_i8, 1)
                    v.tensor_tensor(GA[:], V8[:, :, 0], V8[:, :, 1], ALU.subtract).then_inc(s_gd, 1)
                    dve.wait_ge(s_i8, n + 1)
                    v.tensor_copy(I8f[:], I8[:, :, 0:2]).then_inc(s_if, 1)
                    dve.wait_ge(s_if, n + 1)
                    for a in range(2):
                        v.tensor_tensor(OH[:, a], iota8[:].unsqueeze(1).to_broadcast([P, T, E]),
                                        I8f[:, :, a:a + 1].to_broadcast([P, T, E]), ALU.is_equal).then_inc(s_oh, 1)
                    dve.wait_ge(s_th, n + 1)
                    v.tensor_scalar(GT[:, :, 1], GT[:, :, 0], -0.5, 0.5, ALU.mult, ALU.add).then_inc(s_gt, 1)
                    dve.wait_ge(s_gt, 3 * n + 1)
                    v.tensor_scalar(GT[:, :, 0], GT[:, :, 0], 0.5, 0.5, ALU.mult, ALU.add).then_inc(s_gt, 1)
                    dve.wait_ge(s_gt, 3 * n + 2)
                    dve.wait_ge(s_oh, 2 * n + 2)
                    for a in range(2):
                        s = v.tensor_tensor(OH[:, a], OH[:, a], GT[:, :, a:a + 1].to_broadcast([P, T, E]), ALU.mult)
                    s.then_inc(s_gt, 1)
                    dve.wait_ge(s_gt, 3 * n + 3)
                    v.tensor_tensor(GATE[:, bass.ds(n, 1)].rearrange("p n t e -> p (n t) e"), OH[:, 0], OH[:, 1],
                                    ALU.add).then_inc(s_gate, 1)
                    dve.wait_ge(s_gate, n + 1)
                v.memset(held[:], 0.0).then_inc(s_batch, 1)

            for e in range(E + 1):
                a = slice(e * HID, (e + 1) * HID)
                dve.wait_ge(s_stage[e % 2], 16 * (e // 2 + 1))
                v.tensor_copy(E1H[:, a], ST1[:, e % 2, :]).then_inc(s_split_h, 1)
                dve.wait_ge(s_split_h, e + 1)
                v.tensor_tensor(E1L[:, a], ST1[:, e % 2, :], E1H[:, a].bitcast(F32), ALU.subtract).then_inc(s_split, 1)
            nc.vector.sem_inc(s_acc, 2)
            nc.vector.sem_inc(s_do, 4)
            nc.vector.sem_inc(s_st, 16)
            with dve.Fori(0, NG) as n:
                NC = (E + 1) * EC
                for e in range(E + 1):
                    o = (pQKV, pPQ)[e % 2]
                    dve.wait_ge(s_do, n * NC + (e + 1) * EC + 4)
                    if e == 0:
                        v.tensor_copy(ACC[:], o[:]).then_inc(s_acc, 1)
                    else:
                        dve.wait_ge(s_acc, n * (E + 1) + e + 2)
                        for t in range(T):
                            a = slice(t * P, (t + 1) * P)
                            gate = GATE[:, bass.ds(n, 1), t, e - 1:e].rearrange("p n e -> p (n e)")
                            s = v.scalar_tensor_tensor(out=ACC[:, a], in0=o[:, a], scalar=gate, in1=ACC[:, a],
                                                       op0=ALU.mult, op1=ALU.add)
                        s.then_inc(s_acc, 1)
                dve.wait_ge(s_acc, (n + 1) * (E + 1) + 2)
                for t in range(T):
                    s = v.bn_stats(st5[:, t, :], ACC[:, t * D:(t + 1) * D])
                s.then_inc(s_bn5, 1)
                hold(s_bn5, n + 1)
                for t in range(T):
                    s = v.bn_aggr(mv5[:, t, :], st5[:, t, :])
                s.then_inc(s_mv5, 1)
                dve.wait_ge(s_rs5, n + 1)
                for t in range(T):
                    s = v.tensor_scalar(n5[:, t * D:(t + 1) * D], ACC[:, t * D:(t + 1) * D],
                                        mv5[:, t, 0:1], rs5[:, t:t + 1], ALU.subtract, ALU.mult)
                s.then_inc(s_no5, 1)
                dve.wait_ge(s_no5, n + 1)
                dve.wait_ge(s_st, n * 16 + 16)
                v.tensor_tensor(OUT[:], X[:, bass.ds(n, 1), :].rearrange("p n f -> p (n f)"), n5[:],
                                ALU.add).then_inc(s_out, 1)


_OUTS = [((B, S, D), 'float32')]


def kernel(**inputs):
    import numpy as np
    import concourse.bacc as bacc
    from concourse import mybir as mb
    from concourse.bass_utils import run_bass_kernel_spmd as run

    f = lambda n: np.asarray(inputs[n])
    wq, wk, wv = (f(f"L0_attn_{n}").reshape(D, H * K) for n in ("wq", "wk", "wv"))
    arrays = {
        "x": f("L0_attn_x"),
        "wqkv": np.concatenate([wq, wk, wv], axis=1),
        "wqkT": np.stack([wq.T, wk.T], axis=1),
        "omT": np.tile(f("L0_attn_omega").T, (H, 1)),
        "wo": f("L0_attn_wo"),
        "cols": np.concatenate([f("L0_attn_ln1_g")[:, None], f("L0_attn_ln1_b")[:, None],
                                f("L0_attn_b1").reshape(FC, P).T], axis=1),
        "rows": np.concatenate([f(f"L0_attn_{n}") for n in ("ln1_g", "ln1_b", "b2", "ln2_g", "ln2_b")])[None, :],
        "w1": f("L0_attn_w1"),
        "w2": f("L0_attn_w2").reshape(FC, P, D).transpose(1, 0, 2),
        "ew1T": np.concatenate([f("L0_ffn_shared_w1")[None], f("L0_ffn_experts_w1")]).transpose(0, 2, 1),
        "ew2T": np.concatenate([f("L0_ffn_shared_w2")[None], f("L0_ffn_experts_w2")])
                  .reshape(E + 1, D, EC, P).transpose(3, 0, 2, 1).reshape(P, (E + 1) * EC, D),
        "gwT": f("L0_ffn_gate_w").T,
    }
    nc = bacc.Bacc("TRN2", target_bir_lowering=False, num_devices=1)
    feed, args = {}, []
    for name, a in arrays.items():
        a = np.ascontiguousarray(a)
        feed[f"in_{name}"] = a
        args.append(nc.dram_tensor(f"in_{name}", a.shape, mb.dt.from_np(a.dtype), kind="ExternalInput").ap())
    for i, (shape, dtype) in enumerate(_OUTS):
        args.append(nc.dram_tensor(f"out_{i}", shape, mb.dt.from_np(np.dtype(dtype)), kind="ExternalOutput").ap())
    build(nc, *args)
    r = run(nc, [feed], core_ids=[0])
    return r.results[0]["out_0"]
```

```python
from contextlib import ExitStack

import concourse.bass as bass
from concourse import mybir

F32 = mybir.dt.float32
F32R = mybir.dt.float32r
F16 = mybir.dt.float16
BF16 = mybir.dt.bfloat16
I32 = mybir.dt.int32
U32 = mybir.dt.uint32
ALU = mybir.AluOpType
ACT = mybir.ActivationFunctionType
AX_X = mybir.AxisListType.X

P = 128
D = 128
B, S = 2, 2048
T = 4
GW = T * P
GB = S // GW
NG = B * GB
NT = GB * T
H, K, M = 16, 8, 32
HM = H * M
CH = HM // P
HC = H // CH
KE = K + 1
VW = H * KE
FF = 512
FC = FF // P
E = 8
HID = 512
EC = HID // P
SCALE = float(K) ** -0.25
DELTA = 1e-6 * float(M) ** 0.5
EPS_IN, EPS_OUT = 1e-5, 1e-6
LN_EPS = [EPS_IN, EPS_OUT, EPS_OUT, EPS_IN, EPS_IN]

TOPK = 2
BW = 2 * P
UNROLL = 8
NBLK = -(-(TOPK * B * S // BW + E - 1) // UNROLL) * UNROLL
CAP = B * S + BW
SPARE = S * TOPK
XROWS = E * CAP + SPARE
RESULTS = TOPK * B * S
YROWS = RESULTS + E * BW + SPARE
RW = D + 4
GATE_AT, ID_AT = D, D + 1
assert NBLK * BW - RESULTS <= SPARE


def build(nc, xs, ys, x, wqkv, wqkT, omT, wo, cols, rows, w1, w2, ew1T, ew2T, gwT, out):
    x_v = x.rearrange("b (g p t) d -> (b g) p (t d)", p=P, t=T)
    out_v = out.rearrange("b (g p t) d -> (b g) p (t d)", p=P, t=T)
    ys_v = ys[0:RESULTS].rearrange("(n p c) d -> n p (c d)", p=P, c=T * TOPK)

    with ExitStack() as ctx:
        def sb(name, shape, dt=F32):
            return ctx.enter_context(nc.sbuf_tensor(name, shape, dt))

        def psum(name):
            return ctx.enter_context(nc.psum_tensor(name, [P, 512], F32))

        def sem(name):
            return ctx.enter_context(nc.semaphore(name))

        X = sb("X", [P, NG, GW])
        XN = sb("XN", [P, GB, GW])
        XTH = sb("XTH", [P, 2, GW], F32R)
        XTL = sb("XTL", [P, 2, GW], F32R)
        WA = H * K * 3 + 2 * HM
        WH = sb("WH", [P, WA], F32R)
        WL = sb("WL", [P, WA], F32R)
        wo_s = sb("wo_s", [P, P])
        cols_s = sb("cols_s", [P, 2 + FC])
        rows_s = sb("rows_s", [P, 5, P])
        b12 = sb("b12", [P, P])
        w1_s = sb("w1_s", [P, FF])
        w2_s = sb("w2_s", [P, FC, P])
        gwT_s = sb("gwT_s", [P, E])
        ident = sb("ident", [P, P])
        headmask = sb("headmask", [P, H])
        kvmask = sb("kvmask", [P, HC])
        selQ = sb("selQ", [64, HM], F32R)
        selK = sb("selK", [64, HM], F32R)
        delta = sb("delta", [P, P])
        halves = sb("halves", [P, T])
        eps = sb("eps", [P, 2, T])
        held = sb("held", [P, 3])
        st = sb("st", [P, 5, GB, T, 6])
        mv = sb("mv", [P, 5, GB, T, 2])
        ve = sb("ve", [P, 5, GB, T])
        rs = sb("rs", [P, 5, GB, T])
        SQ = sb("SQ", [P, 2, 2 * D])
        XFT = SQ[:].rearrange("p a d -> p (a d)")
        VX = sb("VX", [P, 3, H, KE])
        MX = sb("MX", [P, 2, 2, H])
        SS = sb("SS", [P, 2, 2, H])
        CC = sb("CC", [P, 2, 2, H])
        CHL = sb("CHL", [P, 2, 4, 2, H], F32R)
        CT = sb("CT", [64, 2, GW], F32R)
        PK = sb("PK", [P, 2, HM])
        PQT = sb("PQT", [P, GB, CH, GW])
        KVB = sb("KVB", [P, VW])
        DS = sb("DS", [P, VW])
        NB = sb("NB", [P, 2, 2, H, KE])
        RD = sb("RD", [P, 2, 2, H])
        AT = sb("AT", [P, T, H, K])
        ATX = sb("ATX", [P, 2, GW])
        ATT, X1T = ATX[:, 0, :], ATX[:, 1, :]
        MID = sb("MID", [P, 5, GW])
        R1, N1, X2, R2, NY = (MID[:, i, :] for i in range(5))
        HT = sb("HT", [P, FC, GW])
        XFH = sb("XFH", [P, NG, GW], F16)
        XFL = sb("XFL", [P, NG, GW], F16)
        iota8 = sb("iota8", [P, E])
        LG = sb("LG", [P, T, E])
        V8 = sb("V8", [P, T, 8])
        I8 = sb("I8", [P, T, 8], U32)
        I8f = sb("I8f", [P, T, TOPK])
        GA = sb("GA", [P, T])
        TH = sb("TH", [P, T])
        OH = sb("OH", [P, TOPK, T, E])
        OHS = sb("OHS", [P, T, E], BF16)
        POS = sb("POS", [P, T, E])
        OHP = sb("OHP", [P, TOPK, T, E])
        SLf = sb("SLf", [P, T, TOPK])
        SLOT = sb("SLOT", [P, GB, T, TOPK], U32)
        BASE = sb("BASE", [P, E])
        IDS = sb("IDS", [P, T, TOPK])
        PL = sb("PL", [P, GB, T, TOPK, RW])
        before = sb("before", [P, P], BF16)
        ones_b = sb("ones_b", [P, P], BF16)
        filslot = sb("filslot", [P, E], U32)
        ecap = sb("ecap", [P, E])
        leq = sb("leq", [P, E, E])
        NK = B * S // BW
        kb = sb("kb", [P, NK])
        CNT = sb("CNT", [P, E])
        NBK = sb("NBK", [P, E])
        CE = sb("CE", [P, E])
        jb = sb("jb", [P, NBLK])
        IND, INB = (HT[:, i, 0:NBLK * E].rearrange("p (j e) -> p j e", e=E) for i in range(2))
        GTK = HT[:, 2, 0:E * NK].rearrange("p (e k) -> p e k", e=E)
        CEM = HT[:, 3, 0:E * E].rearrange("p (a e) -> p a e", a=E)
        EJ = sb("EJ", [P, NBLK])
        CSJ = sb("CSJ", [P, NBLK])
        RO = sb("RO", [P, NBLK])
        ROWf = sb("ROWf", [P, NBLK])
        ROW = sb("ROW", [P, NBLK], U32)
        EW = sb("EW", [P, NBLK], U32)
        ssum = sb("ssum", [P, 1])
        stot = sb("stot", [P, 1])
        hexp = sb("hexp", [P, 1], U32)
        wscale = sb("wscale", [P, 1])
        wunscale = sb("wunscale", [P, 1])
        E1H = sb("E1H", [P, E + 1, HID], F16)
        E1L = sb("E1L", [P, E + 1, HID], F16)
        E2 = sb("E2", [P, E + 1, EC, D])
        XBH, XBL = (PK[:, i, :].bitcast(F16)[:, 0:2 * BW].rearrange("p (q s) -> p q s", q=2) for i in range(2))
        st5 = sb("st5", [P, 2, T, 6])
        mv5 = sb("mv5", [P, 2, T, 2])
        ve5 = sb("ve5", [P, 2, T])
        rs5 = sb("rs5", [P, 2, T])

        pq = PQT[:].rearrange("p g c f -> p (g c f)")

        def parts(flat, *widths):
            at = 0
            for w in widths:
                yield flat[:, at:at + w]
                at += w

        EW1, W_f, wqkT_f, omT_s, omBD_f, ones, sel_a, sel_b = parts(
            pq, (E + 1) * HID, 3 * D, 2 * P, M, HM, HM, HM, HM)
        wqkT_s = wqkT_f.rearrange("p (i d) -> p i d", i=2)
        omBD = omBD_f.rearrange("p (h m) -> p h m", h=H)
        SH = pq[:, 0:NG * GW].rearrange("p (n f) -> p n f", n=NG)
        XS = [v.rearrange("p (t w) -> p t w", t=2) for v in parts(pq[:, NG * GW:], *[2 * RW] * UNROLL)]
        mid = MID[:].rearrange("p a f -> p (a f)")
        Y = [v.rearrange("p (t d) -> p t d", t=2) for v in parts(mid, *[2 * D] * UNROLL)]
        FIL = mid[:, 0:E * 2 * RW].rearrange("p (e a w) -> p e a w", e=E, a=2)
        YC = [mid[:, 0:2 * GW], mid[:, 2 * GW:4 * GW]]
        ST1 = ATX
        HTS = [HT, XN]
        AY = [HT[:, 0, :], HT[:, 1, :]]
        ACC = [HT[:, 2, :], HT[:, 3, :]]
        N5 = [XN[:, 0, :], XN[:, 1, :]]
        OUT = [XN[:, 2, :], XN[:, 3, :]]

        pT, pQKV, pPQ = psum("pT"), psum("pQKV"), psum("pPQ")
        pPK = [psum("pPK0"), psum("pPK1")]
        pF = [psum("pF0"), psum("pF1")]
        pKV = psum("pKV")

        s_x = [sem(f"x_loaded{g}") for g in range(GB)]
        s_w, s_ew1, s_w2 = sem("weights_loaded"), sem("expert_w1_loaded"), sem("expert_w2_loaded")
        s_stage = [sem(f"staged{i}") for i in range(2)]
        s_const, s_prep_p, s_prep_v = sem("pool_constants"), sem("prep_products"), sem("prep_by_dve")
        s_batch = sem("batch_done")
        s_bn, s_mv, s_ve, s_rs, s_no = ([sem(f"{n}{j}") for j in range(5)] for n in (
            "bn_stats", "mean_var", "var_eps", "rstd", "normed"))
        s_xT, s_xh, s_xl = sem("xn_turned"), sem("xn_hi"), sem("xn_lo")
        s_qkv, s_pk, s_pq = sem("qkv_ready"), sem("pk_raw"), sem("pq_raw")
        s_sq, s_vx = sem("squares"), sem("v_copied")
        s_mxk, s_mxq, s_ss, s_cc, s_ch, s_cl = (sem(n) for n in (
            "max_k", "max_q", "sq_sum", "c_sum", "c_hi", "c_lo"))
        s_cT, s_ct, s_pkb, s_ek = sem("c_turned"), sem("c_copied"), sem("pk_biased"), sem("exp_k")
        s_kv, s_kvall, s_fm, s_eq = sem("kv_step"), sem("kv_masked"), sem("pq_biased"), sem("exp_q")
        s_ds, s_dsc = sem("dsum"), sem("dsum_copied")
        s_num, s_nb, s_rd, s_at = sem("num_den"), sem("num_den_copied"), sem("den_recip"), sem("attn")
        s_aT, s_att, s_wo, s_r1 = sem("attn_turned"), sem("attn_copied"), sem("wo_done"), sem("res1")
        s_n1g, s_x2 = sem("n1_times_g"), sem("x2_ready")
        s_nT, s_x1t, s_up, s_ge, s_dn, s_r2 = (sem(n) for n in (
            "n1_turned", "x1t", "up_done", "gelu_done", "down_done", "res2"))
        s_n2g, s_y2, s_x1 = sem("n2_times_g"), sem("y_ready"), sem("x1_ready")
        s_fT, s_xft, s_xfh, s_xfl, s_lg, s_lgc = (sem(n) for n in (
            "xf_turned", "xf_copied", "xf_hi", "xf_lo", "logits", "logits_copied"))
        s_v8, s_i8, s_if, s_gd, s_th, s_gt, s_oh, s_ohs = (sem(n) for n in (
            "top8", "top8_index", "index_float", "top2_gap", "tanh_gap", "gates", "onehots", "onehot_sum"))
        s_pid, s_ids, s_cpy = sem("row_ids"), sem("ids_next"), sem("row_copied")
        s_rt, s_pos, s_base, s_ohp, s_slf, s_slot = (sem(n) for n in (
            "routed", "positions", "base_next", "slot_terms", "slot_float", "slots"))
        s_scat = [sem(f"scattered{g}") for g in range(GB)]
        s_tab, s_filz, s_fil, s_fill = sem("table_step"), sem("filler_zero"), sem("filler_rows"), sem("fillers_written")
        s_ssq, s_stot, s_sc = sem("w1_squares"), sem("w1_norm"), sem("scale_step")
        s_eh, s_el = sem("w1_hi"), sem("w1_lo")
        s_su, s_ss1, s_sd, s_sh = sem("shared_up"), sem("shared_silu"), sem("shared_down"), sem("shared_copied")
        s_bx = [sem(f"block_loaded{q}") for q in range(UNROLL)]
        s_bT, s_bh, s_bl, s_u, s_si, s_do, s_y = (sem(n) for n in (
            "block_turned", "block_hi", "block_lo", "block_up", "block_silu", "block_down", "block_result"))
        s_take = sem("result_taken")
        s_ysc = [sem(f"result_scattered{q}") for q in range(UNROLL)]
        s_yc = [sem(f"results_loaded{q}") for q in range(2)]
        s_ya, s_acc, s_bn5, s_mv5, s_ve5, s_rs5, s_no5, s_out = (sem(n) for n in (
            "routed_sum", "all_sum", "bn5", "mv5", "ve5", "rs5", "no5", "out_ready"))
        s_st = [sem(f"stored{q}") for q in range(2)]

        NLOADS = 9
        NCONST = 34
        NPREP = 13

        def wait(eng, s, value):
            if not isinstance(value, int) or value > 0:
                eng.wait_ge(s, value)

        STAGGER, STAGES = 3, 16

        def pipeline(stage):
            for step in range(STAGGER * (GB - 1) + STAGES):
                for g in range(GB):
                    if 0 <= step - STAGGER * g < STAGES:
                        stage(g, step - STAGGER * g)

        block = ctx.enter_context(nc.Block())

        @block.sync
        def _(sp):
            sp.dma_start(X[:, 0, :], x_v[0]).then_inc(s_x[0], 16)
            sp.dma_start(wqkT_s, wqkT).then_inc(s_w, 16)
            sp.dma_start(omT_s, omT).then_inc(s_w, 16)
            sp.dma_start(W_f, wqkv).then_inc(s_w, 16)
            sp.dma_start(rows_s[:].rearrange("p v d -> p (v d)"), rows.to_broadcast([P, 5 * P])).then_inc(s_w, 16)
            sp.dma_start(cols_s[:], cols).then_inc(s_w, 16)
            sp.dma_start(gwT_s[:], gwT).then_inc(s_w, 16)
            sp.dma_start(wo_s[:], wo).then_inc(s_w, 16)
            sp.dma_start(w1_s[:], w1).then_inc(s_w, 16)
            sp.dma_start(w2_s[:], w2).then_inc(s_w, 16)
            sp.dma_start(EW1.rearrange("p (e h) -> p e h", e=E + 1), ew1T).then_inc(s_ew1, 16)
            for g in range(1, GB):
                sp.dma_start(X[:, g, :], x_v[g]).then_inc(s_x[g], 16)
            for g in range(GB):
                sp.wait_ge(s_x[g], 16)
                sp.dma_start(X[:, GB + g, :], x_v[GB + g]).then_inc(s_x[g], 16)
            sp.dma_start(E2[:], ew2T).then_inc(s_w2, 16)
            sp.wait_ge(s_batch, B + 1)
            for e in range(2):
                sp.dma_start(ST1[:, e, :], ew1T[:, e, :]).then_inc(s_stage[e], 16)
            sp.wait_ge(s_fil, 1)
            sp.wait_ge(s_tab, 2)
            for e in range(E):
                row = sp.value_load(filslot[0:1, e:e + 1], min_val=0, max_val=XROWS - BW)
                sp.dma_start(xs[bass.ds(row, BW)].rearrange("(p a) w -> p a w", a=2), FIL[:, e]).then_inc(s_fill, 16)
            for e in range(2, E + 1):
                sp.wait_ge(s_el, e - 1)
                sp.dma_start(ST1[:, e % 2, :], ew1T[:, e, :]).then_inc(s_stage[e % 2], 16)
            sp.wait_ge(s_fill, 16 * E)
            for g in range(GB):
                sp.wait_ge(s_scat[g], 16 * TOPK * T * (B + 1))
            sp.wait_ge(s_tab, 13)

            def load_blocks(j):
                for q in range(UNROLL):
                    row = sp.value_load(ROW[0:1, bass.ds(j * UNROLL + q, 1)], min_val=0, max_val=XROWS - BW)
                    wait(sp, s_ysc[q], j * 32)
                    sp.dma_start(XS[q], xs[bass.ds(row, BW)].rearrange("(p a) w -> p a w", a=2)).then_inc(s_bx[q], 16)

            load_blocks(0)
            with sp.Fori(1, NBLK // UNROLL) as j:
                load_blocks(j)
            for q in range(UNROLL):
                sp.wait_ge(s_ysc[q], 32 * (NBLK // UNROLL))

            def load_results(i):
                for q in range(2):
                    wait(sp, s_ya, i * 2 + q - 1)
                    sp.dma_start(YC[q], ys_v[bass.ds(i * 2 + q, 1)].rearrange("n p f -> (n p) f")).then_inc(s_yc[q], 16)

            load_results(0)
            with sp.Fori(1, NG // 2) as i:
                load_results(i)

        @block.gpsimd
        def _(pool):
            eng = nc.gpsimd
            count = [0]

            def const(ins):
                count[0] += 1
                ins.then_inc(s_const, 1)

            def settle():
                pool.wait_ge(s_const, count[0])

            const(eng.memset(ones, 1.0))
            const(eng.memset(sel_a, -1.0))
            const(eng.memset(eps[:, 0, :], EPS_IN))
            const(eng.memset(eps[:, 1, :], EPS_OUT))
            const(eng.memset(halves[:], -0.5))
            settle()
            const(eng.affine_select(out=ident[:], in_=ones[:, 0:P], compare_op=ALU.is_equal, fill=0.0, base=0,
                                    pattern=[[-1, P]], channel_multiplier=1))
            const(eng.affine_select(out=headmask[:], in_=ones[:, 0:H], compare_op=ALU.is_ge, fill=0.0, base=0,
                                    pattern=[[-K, H]], channel_multiplier=1))
            const(eng.affine_select(out=kvmask[:], in_=ones[:, 0:HC], compare_op=ALU.is_ge, fill=0.0, base=0,
                                    pattern=[[-M, HC]], channel_multiplier=1))
            settle()
            const(eng.affine_select(out=headmask[:], in_=headmask[:], compare_op=ALU.is_ge, fill=0.0, base=K - 1,
                                    pattern=[[K, H]], channel_multiplier=-1))
            const(eng.affine_select(out=kvmask[:], in_=kvmask[:], compare_op=ALU.is_ge, fill=0.0, base=M - 1,
                                    pattern=[[M, HC]], channel_multiplier=-1))
            def selector(dst, offset):
                const(eng.affine_select(out=dst[0:64].rearrange("p (h m) -> p h m", m=M),
                                        in_=sel_a[0:64].rearrange("p (h m) -> p h m", m=M),
                                        compare_op=ALU.is_equal, fill=0.0, base=-offset,
                                        pattern=[[-1, H], [0, M]], channel_multiplier=1))

            sel4 = [HT[:, i, :] for i in range(4)]
            for i in range(4):
                selector(sel4[i], i * H)
            settle()
            const(eng.tensor_tensor(sel_b[0:64], sel4[0][0:64], sel4[1][0:64], ALU.add))
            const(eng.tensor_tensor(MID[0:64, 0, :], sel4[2][0:64], sel4[3][0:64], ALU.add))
            const(eng.memset(delta[:], DELTA))
            const(eng.memset(VX[:], 1.0))
            settle()
            ints = HT[:, 0, 0:E + E + NK + NBLK].bitcast(I32)
            i8, iec, ikb, ijb = parts(ints, E, E, NK, NBLK)
            ids = HT[:, 1, 0:T * TOPK].bitcast(I32)
            const(eng.iota(i8, pattern=[[1, E]], base=0, channel_multiplier=0))
            const(eng.iota(iec, pattern=[[CAP, E]], base=0, channel_multiplier=0))
            const(eng.iota(ikb, pattern=[[BW, NK]], base=0, channel_multiplier=0))
            const(eng.iota(ijb, pattern=[[1, NBLK]], base=0, channel_multiplier=0))
            const(eng.iota(ids, pattern=[[TOPK, T], [1, TOPK]], base=0, channel_multiplier=T * TOPK))
            const(eng.memset(ones_b[:], 1.0))
            const(eng.memset(PL[:], 0.0))
            spare = [[TOPK * P, GB * T], [P, TOPK]]
            const(eng.iota(SLOT[:].rearrange("p g t a -> p (g t) a").bitcast(I32), pattern=spare, base=E * CAP,
                           channel_multiplier=1))
            settle()
            const(eng.iota(PL[:].rearrange("p g t a w -> p (g t) a w")[:, :, :, ID_AT].bitcast(I32), pattern=spare,
                           base=RESULTS + E * BW, channel_multiplier=1))
            for dst, i in ((iota8, i8), (ecap, iec), (kb, ikb), (jb, ijb)):
                const(eng.tensor_copy(dst[:], i))
            const(eng.tensor_copy(IDS[:].rearrange("p t a -> p (t a)"), ids))
            const(eng.affine_select(out=before[:], in_=ones_b[:], compare_op=ALU.is_gt, fill=0.0, base=0,
                                    pattern=[[1, P]], channel_multiplier=-1))
            const(eng.affine_select(out=leq[:], in_=ones[:, 0:E * E].rearrange("p (a b) -> p a b", a=E),
                                    compare_op=ALU.is_ge, fill=0.0, base=0, pattern=[[1, E], [-1, E]],
                                    channel_multiplier=0))
            assert count[0] == NCONST, count
            pool.wait_ge(s_w, 16 * NLOADS)
            eng.tensor_tensor(b12[:], rows_s[:, 1, :], rows_s[:, 2, :], ALU.add).then_inc(s_const, 1)
            pool.wait_ge(s_ssq, 1)
            eng.partition_all_reduce(stot[:], ssum[:], P, bass.bass_isa.ReduceOp.add).then_inc(s_stot, 1)

            def hold(s, value, at=1):
                pool.wait_ge(s, value)
                return eng.tensor_tensor(held[:, at:at + 1], halves[:, 0:1], halves[:, 1:2], ALU.add)

            def rstd(b, j, g):
                pool.wait_ge(s_mv[j], b * GB + g + 1)
                eng.tensor_tensor(ve[:, j, g, :], mv[:, j, g, :, 1], eps[:, int(LN_EPS[j] == EPS_OUT), :],
                                  ALU.add).then_inc(s_ve[j], 1)
                pool.wait_ge(s_ve[j], b * GB + g + 1)
                eng.tensor_tensor(rs[:, j, g, :], ve[:, j, g, :], halves[:], ALU.pow).then_inc(s_rs[j], 1)

            def affine(b, g, s_in, src, dst, gain, bias, s_mid, s_end):
                pool.wait_ge(s_in, b * GB + g + 1)
                d, n = (v.rearrange("p (t d) -> p t d", t=T) for v in (dst, src))
                eng.tensor_tensor(d, n, gain.unsqueeze(1).to_broadcast([P, T, D]), ALU.mult).then_inc(s_mid, 1)
                pool.wait_ge(s_mid, b * GB + g + 1)
                eng.tensor_tensor(d, d, bias.unsqueeze(1).to_broadcast([P, T, D]), ALU.add).then_inc(s_end, 1)

            def scatter_rows(g):
                for t in range(T):
                    for a in range(TOPK):
                        eng.indirect_dma_start(xs, bass.IndirectOffsetOnAxis(SLOT[:, g, t, a:a + 1], 0),
                                               PL[:, g, t, a, :], None).then_inc(s_scat[g], 16)

            pool.wait_ge(s_const, NCONST + 1)
            with pool.Fori(0, B) as b:
                for g in range(GB):
                    rstd(b, 0, g)
                    scatter_rows(g)

                def stage(g, k):
                    n = b * GB + g
                    if k == 2:
                        rstd(b, 1, g)
                    if k == 3:
                        if g:
                            pool.wait_ge(s_r2, b * GB + g)
                        affine(b, g, s_no[1], N1, X2, rows_s[:, 0, :], b12[:], s_n1g, s_x2)
                    if k == 6:
                        rstd(b, 2, g)
                    if k == 7:
                        affine(b, g, s_no[2], NY, NY, rows_s[:, 3, :], rows_s[:, 4, :], s_n2g, s_y2)
                    if k == 8:
                        rstd(b, 3, g)
                    if k == 9:
                        xg = X[:, bass.ds(n, 1), :].rearrange("p n f -> p (n f)")
                        pool.wait_ge(s_no[3], n + 1)
                        eng.tensor_tensor(xg, xg, NY, ALU.add).then_inc(s_x1, 1)
                    if k == 10:
                        rstd(b, 4, g)
                    if k == 11:
                        hold(s_no[4], n + 1)
                        eng.tensor_copy(PL[:, g, :, 1, 0:D], PL[:, g, :, 0, 0:D]).then_inc(s_cpy, 1)

                pipeline(stage)
                pool.wait_ge(s_slot, (b + 1) * GB)
                pool.wait_ge(s_cpy, (b + 1) * GB)

            pool.wait_ge(s_batch, B + 1)
            eng.memset(FIL, 0.0).then_inc(s_filz, 1)
            pool.wait_ge(s_filz, 1)
            eng.iota(FIL[:, :, :, ID_AT].bitcast(I32), pattern=[[BW, E], [1, 2]], base=RESULTS,
                     channel_multiplier=2).then_inc(s_fil, 1)
            for g in range(GB):
                scatter_rows(g)

            def scatter_results(j):
                for q in range(UNROLL):
                    pool.wait_ge(s_take, j * UNROLL + q + 1)
                    hold(s_y, j * UNROLL + q + 1, at=2).then_inc(s_take, 1)
                    for t in range(2):
                        eng.indirect_dma_start(ys, bass.IndirectOffsetOnAxis(XS[q][:, t, ID_AT:ID_AT + 1].bitcast(U32), 0),
                                               Y[q][:, t, :], None).then_inc(s_ysc[q], 16)

            eng.memset(held[:, 2:3], 0.0).then_inc(s_take, 1)
            with pool.Fori(0, NBLK // UNROLL) as j:
                scatter_results(j)

            with pool.Fori(0, NG // 2) as i:
                for q in range(2):
                    pool.wait_ge(s_yc[q], i * 16 + 16)
                    y = YC[q].rearrange("p (t a d) -> p t a d", t=T, a=TOPK)
                    eng.tensor_tensor(AY[q].rearrange("p (t d) -> p t d", t=T), y[:, :, 0], y[:, :, 1],
                                      ALU.add).then_inc(s_ya, 1)
                for q in range(2):
                    n = i * 2 + q
                    pool.wait_ge(s_mv5, n + 1)
                    eng.tensor_tensor(ve5[:, q], mv5[:, q, :, 1], eps[:, 0, :], ALU.add).then_inc(s_ve5, 1)
                    pool.wait_ge(s_ve5, n + 1)
                    eng.tensor_tensor(rs5[:, q], ve5[:, q], halves[:], ALU.pow).then_inc(s_rs5, 1)

        @block.tensor
        def _(pe):
            def three(o, a, b_, stop=True):
                nc.tensor.matmul(o, a[0], b_[0], start=True, stop=False)
                nc.tensor.matmul(o, a[0], b_[1], start=False, stop=False)
                return nc.tensor.matmul(o, a[1], b_[0], start=False, stop=stop)

            def turn(bank, src):
                for t in range(T):
                    m = nc.tensor.transpose(bank[:, t * P:(t + 1) * P], src(t), ident[:])
                return m

            pe.wait_ge(s_prep_v, 2)
            for i in range(2):
                nc.tensor.matmul(pF[i][:], wqkT_s[:, i, :], omBD_f, start=True, stop=True).then_inc(s_prep_p, 1)
            pe.wait_ge(s_prep_v, NPREP)

            def turn_xn(b, g):
                pe.wait_ge(s_no[0], b * GB + g + 1)
                turn(pT, lambda t: XN[:, g, t * P:(t + 1) * P]).then_inc(s_xT, 1)

            w = lambda a, n: [v[:, a:a + n] for v in (WH, WL)]

            def xt(i):
                return [v[:, i // T % 2, i % T * P:(i % T + 1) * P] for v in (XTH, XTL)]

            def qkv_pk(b, i):
                if i % T == 0:
                    pe.wait_ge(s_xl, b * GB + i // T + 1)
                if i:
                    pe.wait_ge(s_vx, b * NT + i)
                three(pQKV[:, 0:3 * D], xt(i), w(0, 3 * D)).then_inc(s_qkv, 1)
                if i >= 2:
                    pe.wait_ge(s_ek, b * NT + i - 1)
                three(pPK[i % 2][:], xt(i), w(3 * D + HM, HM)).then_inc(s_pk, 1)

            def pq(b, i):
                if i:
                    pe.wait_ge(s_mxq, b * NT + i)
                three(pPQ[:], xt(i), w(3 * D, HM)).then_inc(s_pq, 1)

            def turn_bias(b, i):
                g, t = i // T, i % T
                if t == 2 and g + 1 < GB:
                    pe.wait_ge(s_xl, b * GB + g + 2)
                pe.wait_ge(s_cl, b * NT + i + 1)
                nc.tensor.transpose(pT[:, 0:P], CHL[:, i % 2].rearrange("p a c h -> p (a c h)").bitcast(F32),
                                    ident[:]).then_inc(s_cT, 1)

            def bias_k(b, i):
                g, t = i // T, i % T
                pe.wait_ge(s_ct, b * NT + i + 1)
                pe.wait_ge(s_mxk, b * NT + i + 1)
                nc.tensor.matmul(pPK[i % 2][:], CT[:, g % 2, t * P:(t + 1) * P], selK[:],
                                 start=False, stop=True, skip_group_check=True).then_inc(s_pkb, 1)

            def sum_kv(b, i):
                pe.wait_ge(s_ek, b * NT + i + 1)
                pe.wait_ge(s_vx, b * NT + i + 1)
                v = VX[:, i % 3].rearrange("p h k -> p (h k)")
                nc.tensor.matmul(pKV[:, 0:VW], delta[:], v, start=(i == 0), stop=False, skip_group_check=True)
                for c in range(CH):
                    w = HC * KE
                    m = nc.tensor.matmul(pKV[:, c * w:(c + 1) * w], PK[:, i % 2, c * P:(c + 1) * P],
                                         v[:, c * w:(c + 1) * w], start=False, stop=(i == NT - 1 and c == CH - 1),
                                         skip_group_check=True)
                m.then_inc(s_kv, 1)

            def features_q(b, g):
                xt = [v[:, g % 2, :] for v in (XTH, XTL)]
                for c in range(CH):
                    if g * CH + c >= 2:
                        pe.wait_ge(s_eq, b * GB * CH + g * CH + c - 1)
                    w = [v[:, 3 * D + c * P:3 * D + (c + 1) * P] for v in (WH, WL)]
                    three(pF[c % 2][:], w, xt, stop=False)
                    nc.tensor.matmul(pF[c % 2][:], selQ[:, c * P:(c + 1) * P], CT[:, g % 2, :],
                                     start=False, stop=True).then_inc(s_fm, 1)

            with pe.Fori(0, B) as b:
                pe.wait_ge(s_batch, b + 1)
                turn_xn(b, 0)
                for i in range(NT + 2):
                    if i < NT:
                        qkv_pk(b, i)
                    if 1 <= i <= NT:
                        turn_bias(b, i - 1)
                    if i < NT:
                        pq(b, i)
                    if 1 <= i <= NT:
                        bias_k(b, i - 1)
                    if i >= 2:
                        sum_kv(b, i - 2)
                    if i % T == 1 and i > 1:
                        features_q(b, i // T - 1)
                    if i % T == 2 and i < NT - T:
                        turn_xn(b, i // T + 1)
                pe.wait_ge(s_kvall, b + 1)
                nc.tensor.matmul(pT[:, 0:VW], delta[:], KVB[:], start=True, stop=True).then_inc(s_ds, 1)
                pe.wait_ge(s_dsc, b + 1)
                pe.wait_ge(s_eq, (b + 1) * GB * CH)

                def stage(g, k):
                    n = b * GB + g
                    if k == 0:
                        if g:
                            pe.wait_ge(s_nb, 2 * n)
                        w = HC * KE
                        for t in range(T):
                            for c in range(CH):
                                a = (t % 2) * VW + c * w
                                m = nc.tensor.matmul(pF[t // 2][:, a:a + w], PQT[:, g, c, t * P:(t + 1) * P],
                                                     KVB[:, c * w:(c + 1) * w], start=True, stop=True)
                            if t % 2:
                                m.then_inc(s_num, 1)
                    if k == 1:
                        if g:
                            pe.wait_ge(s_x1t, n)
                        pe.wait_ge(s_at, 2 * n + 2)
                        turn(pT, lambda t: AT[:, t].rearrange("p h k -> p (h k)")).then_inc(s_aT, 1)
                    if k == 2:
                        if g:
                            pe.wait_ge(s_r1, n)
                        pe.wait_ge(s_att, n + 1)
                        for t in range(T):
                            m = nc.tensor.matmul(pPQ[:, t * P:(t + 1) * P], ATT[:, t * P:(t + 1) * P], wo_s[:],
                                                 start=True, stop=True)
                        m.then_inc(s_wo, 1)
                    if k == 4:
                        pe.wait_ge(s_no[1], n + 1)
                        turn(pT, lambda t: N1[:, t * P:(t + 1) * P]).then_inc(s_nT, 1)
                    if k == 5:
                        pe.wait_ge(s_x1t, n + 1)
                        for c in range(FC):
                            if g * FC + c >= 2:
                                pe.wait_ge(s_ge, n * FC + c - 1)
                            nc.tensor.matmul(pPK[c % 2][:], w1_s[:, c * P:(c + 1) * P], X1T,
                                             start=True, stop=True).then_inc(s_up, 1)
                    if k == 6:
                        if g:
                            pe.wait_ge(s_r2, n)
                        pe.wait_ge(s_ge, (n + 1) * FC)
                        for t in range(T):
                            for c in range(FC):
                                m = nc.tensor.matmul(pQKV[:, t * P:(t + 1) * P], HT[:, c, t * P:(t + 1) * P],
                                                     w2_s[:, c, :], start=(c == 0), stop=(c == FC - 1))
                        m.then_inc(s_dn, 1)
                    if k == 12:
                        pe.wait_ge(s_no[4], n + 1)
                        turn(pKV, lambda t: PL[:, g, t, 0, 0:D]).then_inc(s_fT, 1)
                    if k == 13:
                        pe.wait_ge(s_xfl, n + 1)
                        pe.wait_ge(s_xft, n + 1)
                        for t in range(T):
                            m = nc.tensor.matmul(pKV[:, t * E:(t + 1) * E], XFT[:, t * P:(t + 1) * P], gwT_s[:],
                                                 start=True, stop=True)
                        m.then_inc(s_lg, 1)
                    if k == 14:
                        pe.wait_ge(s_lgc, n + 1)
                        pe.wait_ge(s_ohs, n + 1)
                        r = pKV[:, 64:64 + T * E]
                        nc.tensor.matmul(r, before[:], OHS[:].rearrange("p t e -> p (t e)"), start=True, stop=False,
                                         skip_group_check=True)
                        for t in range(T - 1):
                            nc.tensor.matmul(r[:, (t + 1) * E:].rearrange("p (t e) -> p t e", e=E), ones_b[:],
                                             OHS[:, t:t + 1, :].to_broadcast([P, T - 1 - t, E]),
                                             start=False, stop=(t == T - 2), skip_group_check=True)
                        for t in range(T):
                            m = nc.tensor.matmul(pKV[:, 128:128 + E], ones_b[:], OHS[:, t, :], start=(t == 0),
                                                 stop=(t == T - 1), skip_group_check=True)
                        m.then_inc(s_rt, 1)
                        pe.wait_ge(s_base, n + 1)

                pipeline(stage)

            banks = [pF[0], pF[1], pPK[0], pPK[1]]
            pe.wait_ge(s_batch, B + 1)
            pe.wait_ge(s_el, 1)
            pe.wait_ge(s_w2, 16)

            def shared_up(i, q):
                n = i * 2 + q
                xf = [v[:, bass.ds(n, 1), :].rearrange("p n f -> p (n f)") for v in (XFH, XFL)]
                for c in range(EC):
                    wait(pe, s_ss1, (n - 1) * EC + c + 1)
                    w = [v[:, 0, c * P:(c + 1) * P] for v in (E1H, E1L)]
                    three(banks[c][:], w, xf).then_inc(s_su, 1)

            def shared_down(i, q):
                n = i * 2 + q
                wait(pe, s_sh, n - 1)
                pe.wait_ge(s_ss1, (n + 1) * EC)
                o = (pQKV, pPQ)[q]
                for t in range(T):
                    for c in range(EC):
                        m = nc.tensor.matmul(o[:, t * P:(t + 1) * P], HTS[q][:, c, t * P:(t + 1) * P], E2[:, 0, c, :],
                                             start=(c == 0), stop=(c == EC - 1))
                m.then_inc(s_sd, 1)

            def shared(i):
                shared_up(i, 0)
                shared_up(i, 1)
                shared_down(i, 0)
                shared_down(i, 1)

            shared(0)
            with pe.Fori(1, NG // 2) as i:
                shared(i)

            pe.wait_ge(s_tab, 13)
            pe.wait_ge(s_el, E + 1)
            pe.wait_ge(s_sh, NG)
            turned = [pT, pKV]
            outs = [pQKV, pPQ]

            def turn_block(j, q):
                k = j * UNROLL + q
                wait(pe, s_bl, k - 1)
                pe.wait_ge(s_bx[q], j * 16 + 16)
                for t in range(2):
                    m = nc.tensor.transpose(turned[q % 2][:, t * P:(t + 1) * P], XS[q][:, t, 0:D], ident[:])
                m.then_inc(s_bT, 1)

            def weights_of(j, q):
                return pe.value_load(EW[0:1, bass.ds(j * UNROLL + q, 1)], min_val=0, max_val=E)

            def up_block(j, q, ew):
                for c in range(EC):
                    o = banks[q % 2 * 2 + c // 2][:, c % 2 * BW:(c % 2 + 1) * BW]
                    w = [v[:, bass.ds(ew, 1), c * P:(c + 1) * P].rearrange("p e h -> p (e h)") for v in (E1H, E1L)]
                    m = three(o, w, [XBH[:, q % 2, :], XBL[:, q % 2, :]])
                    if c % 2:
                        m.then_inc(s_u, 1)

            def down_block(j, q, ew):
                k = j * UNROLL + q
                wait(pe, s_y, k - 1)
                pe.wait_ge(s_si, 2 * k + 2)
                h = HT[:, q % 2 * 2:q % 2 * 2 + 2, :].rearrange("p a (c s) -> p (a c) s", s=BW)
                for t in range(2):
                    for c in range(EC):
                        w = E2[:, bass.ds(ew, 1), c, :].rearrange("p e d -> p (e d)")
                        m = nc.tensor.matmul(outs[q % 2][:, t * P:(t + 1) * P], h[:, c, t * P:(t + 1) * P], w,
                                             start=(c == 0), stop=(c == EC - 1))
                m.then_inc(s_do, 1)

            def blocks(j, last):
                for q in range(UNROLL):
                    k = j * UNROLL + q
                    wait(pe, s_si, 2 * k - 2)
                    pe.wait_ge(s_bl, k + 1)
                    if q + 1 < UNROLL:
                        turn_block(j, q + 1)
                    elif not last:
                        turn_block(j + 1, 0)
                    else:
                        nc.tensor.transpose(turned[(q + 1) % 2][:, 0:P], XS[q][:, 0, 0:D], ident[:])
                    up_block(j, q, weights_of(j, q))
                    if q:
                        down_block(j, q - 1, weights_of(j, q - 1))
                    elif not isinstance(j, int) or j:
                        down_block(j - 1, UNROLL - 1, weights_of(j - 1, UNROLL - 1))

            turn_block(0, 0)
            blocks(0, False)
            with pe.Fori(1, NBLK // UNROLL - 1) as j:
                blocks(j, False)
            j = NBLK // UNROLL - 1
            blocks(j, True)
            down_block(j, UNROLL - 1, weights_of(j, UNROLL - 1))

        @block.scalar
        def _(act):
            A = nc.scalar.activation

            def squares(b, i):
                act.wait_ge(s_qkv, b * NT + i + 1)
                if i >= 2:
                    act.wait_ge(s_ss, b * NT + i - 1)
                A(SQ[:, i % 2, :], pQKV[:, 0:2 * D], ACT.Square, scale=SCALE * 0.5 ** 0.5).then_inc(s_sq, 1)
                if i >= 3:
                    act.wait_ge(s_kv, b * NT + i - 2)
                A(VX[:, i % 3, :, 0:K], pQKV[:, 2 * D:3 * D].rearrange("p (h k) -> p h k", k=K),
                  ACT.Copy).then_inc(s_vx, 1)

            def exp_k(b, i):
                g, t = i // T, i % T
                act.wait_ge(s_cT, b * NT + i + 1)
                A(CT[:, g % 2, t * P:(t + 1) * P], pT[0:64, 0:P], ACT.Copy).then_inc(s_ct, 1)
                act.wait_ge(s_pkb, b * NT + i + 1)
                if i >= 2:
                    act.wait_ge(s_kv, b * NT + i - 1)
                A(PK[:, i % 2, :], pPK[i % 2][:], ACT.Exp).then_inc(s_ek, 1)

            def exp_q(b, g):
                for c in range(CH):
                    act.wait_ge(s_fm, (b * GB + g) * CH + c + 1)
                    A(PQT[:, g, c, :], pF[c % 2][:], ACT.Exp).then_inc(s_eq, 1)

            def hi_xn(b, g):
                act.wait_ge(s_xT, b * GB + g + 1)
                A(XTH[:, g % 2, :], pT[:], ACT.Copy).then_inc(s_xh, 1)

            act.wait_ge(s_ew1, 16)
            A(E1H[:].rearrange("p e h -> p (e h)").bitcast(BF16), EW1, ACT.Square, accum_out=ssum[:]).then_inc(s_ssq, 1)
            act.wait_ge(s_const, NCONST)
            with act.Fori(0, B) as b:
                act.wait_ge(s_batch, b + 1)
                hi_xn(b, 0)
                for i in range(NT + 2):
                    if i < NT:
                        squares(b, i)
                    if 1 <= i <= NT:
                        exp_k(b, i - 1)
                    if i % T == 1 and i > 1:
                        exp_q(b, i // T - 1)
                    if i % T == 2 and i < NT - T:
                        hi_xn(b, i // T + 1)

                def stage(g, k):
                    n = b * GB + g
                    if k == 1:
                        if g:
                            act.wait_ge(s_wo, n)
                        act.wait_ge(s_aT, n + 1)
                        A(ATT, pT[:], ACT.Copy).then_inc(s_att, 1)
                    if k == 4:
                        if g:
                            act.wait_ge(s_up, n * FC)
                        act.wait_ge(s_nT, n + 1)
                        A(X1T, pT[:], ACT.Identity, scale=cols_s[:, 0:1], bias=cols_s[:, 1:2]).then_inc(s_x1t, 1)
                    if k == 5:
                        if g:
                            act.wait_ge(s_dn, n)
                        for c in range(FC):
                            act.wait_ge(s_up, n * FC + c + 1)
                            A(HT[:, c, :], pPK[c % 2][:], ACT.Gelu, bias=cols_s[:, 2 + c:3 + c]).then_inc(s_ge, 1)
                    if k == 12:
                        if g:
                            act.wait_ge(s_lg, n)
                        act.wait_ge(s_fT, n + 1)
                        A(XFT, pKV[:], ACT.Copy).then_inc(s_xft, 1)
                        A(XFH[:, bass.ds(n, 1), :].rearrange("p n f -> p (n f)"), pKV[:], ACT.Copy).then_inc(s_xfh, 1)
                    if k == 13:
                        act.wait_ge(s_gd, n + 1)
                        A(TH[:], GA[:], ACT.Tanh, scale=0.5).then_inc(s_th, 1)

                pipeline(stage)

            banks = [pF[0], pF[1], pPK[0], pPK[1]]
            act.wait_ge(s_sc, 3)

            def shared(i):
                for q in range(2):
                    n = i * 2 + q
                    for c in range(EC):
                        if c == 0:
                            wait(act, s_sd, n - 1)
                        act.wait_ge(s_su, n * EC + c + 1)
                        A(HTS[q][:, c, :], banks[c][:], ACT.Silu, scale=wunscale[:]).then_inc(s_ss1, 1)

            shared(0)
            with act.Fori(1, NG // 2) as i:
                shared(i)

            def hi_block(j, q):
                k = j * UNROLL + q
                wait(act, s_u, 2 * k - 2)
                act.wait_ge(s_bT, k + 1)
                A(XBH[:, q % 2, :], (pT, pKV)[q % 2][:, 0:BW], ACT.Copy).then_inc(s_bh, 1)

            def blocks(j, last):
                for q in range(UNROLL):
                    k = j * UNROLL + q
                    if q + 1 < UNROLL:
                        hi_block(j, q + 1)
                    elif not last:
                        hi_block(j + 1, 0)
                    for h in range(2):
                        if h == 0:
                            wait(act, s_do, k - 1)
                        act.wait_ge(s_u, 2 * k + h + 1)
                        A(HT[:, q % 2 * 2 + h, :], banks[q % 2 * 2 + h][:], ACT.Silu, scale=wunscale[:]).then_inc(s_si, 1)

            act.wait_ge(s_sd, NG)
            hi_block(0, 0)
            blocks(0, False)
            with act.Fori(1, NBLK // UNROLL - 1) as j:
                blocks(j, False)
            blocks(NBLK // UNROLL - 1, True)

            def store(i):
                for q in range(2):
                    act.wait_ge(s_out, i * 2 + q + 1)
                    act.dma_start(out_v[bass.ds(i * 2 + q, 1)].rearrange("n p f -> (n p) f"), OUT[q]).then_inc(s_st[q], 16)

            with act.Fori(0, NG // 2) as i:
                store(i)
            for q in range(2):
                act.wait_ge(s_st[q], 16 * (NG // 2))

        @block.vector
        def _(dve):
            v = nc.vector
            prep = [0]

            def prepared(ins):
                prep[0] += 1
                ins.then_inc(s_prep_v, 1)

            dve.wait_ge(s_w, 16 * NLOADS)
            dve.wait_ge(s_const, NCONST)
            prepared(v.tensor_tensor(omBD, omT_s.unsqueeze(1).to_broadcast([P, H, M]),
                                     headmask[:].unsqueeze(2).to_broadcast([P, H, M]), ALU.mult))
            dve.wait_ge(s_prep_v, 1)
            prepared(v.tensor_scalar(omBD_f, omBD_f, SCALE, None, ALU.mult))
            prepared(v.tensor_copy(WH[:, 0:3 * D], W_f))
            prepared(v.tensor_copy(selQ[:], sel_b[0:64]))
            prepared(v.tensor_copy(selK[:], MID[0:64, 0, :]))
            dve.wait_ge(s_prep_v, 3)
            prepared(v.tensor_tensor(WL[:, 0:3 * D], W_f, WH[:, 0:3 * D].bitcast(F32), ALU.subtract))
            for i in range(2):
                a = slice(3 * D + i * HM, 3 * D + (i + 1) * HM)
                dve.wait_ge(s_prep_p, i + 1)
                prepared(v.tensor_copy(WH[:, a], pF[i][:]))
                dve.wait_ge(s_prep_v, prep[0])
                prepared(v.tensor_tensor(WL[:, a], pF[i][:], WH[:, a].bitcast(F32), ALU.subtract))
            prepared(v.memset(CHL[:, :, 2:4].bitcast(F32), 0.0))
            prepared(v.tensor_copy(BASE[:], ecap[:]))
            prepared(v.memset(held[:], 0.0))
            dve.wait_ge(s_stot, 1)
            v.tensor_scalar(hexp[:], stot[:].bitcast(U32), 24, None, ALU.logical_shift_right).then_inc(s_sc, 1)
            dve.wait_ge(s_sc, 1)
            v.tensor_scalar(wscale[:].bitcast(U32), hexp[:], -float(2 ** 23), 204.0 * 2 ** 23,
                            ALU.mult, ALU.add).then_inc(s_sc, 1)
            v.tensor_scalar(wunscale[:].bitcast(U32), hexp[:], float(2 ** 23), 50.0 * 2 ** 23,
                            ALU.mult, ALU.add).then_inc(s_sc, 1)
            dve.wait_ge(s_sc, 3)
            assert prep[0] == NPREP, prep
            dve.wait_ge(s_prep_v, prep[0])

            def hold(s, value):
                dve.wait_ge(s, value)
                v.memset(held[:, 0:1], 0.0)

            def stats(b, j, g, src):
                for t in range(T):
                    s = v.bn_stats(st[:, j, g, t, :], src[:, t * D:(t + 1) * D])
                s.then_inc(s_bn[j], 1)
                hold(s_bn[j], b * GB + g + 1)
                for t in range(T):
                    s = v.bn_aggr(mv[:, j, g, t, :], st[:, j, g, t, :])
                s.then_inc(s_mv[j], 1)

            def norm(b, j, g, dst, src):
                dve.wait_ge(s_rs[j], b * GB + g + 1)
                for t in range(T):
                    s = v.tensor_scalar(dst(t), src[:, t * D:(t + 1) * D],
                                        mv[:, j, g, t, 0:1], rs[:, j, g, t:t + 1], ALU.subtract, ALU.mult)
                s.then_inc(s_no[j], 1)

            def tiles(buf):
                return lambda t: buf[:, t * D:(t + 1) * D]

            def lo_xn(b, g):
                dve.wait_ge(s_xh, b * GB + g + 1)
                v.tensor_tensor(XTL[:, g % 2, :], pT[:], XTH[:, g % 2, :].bitcast(F32),
                                ALU.subtract).then_inc(s_xl, 1)

            def row(buf, n):
                return buf[:, bass.ds(n, 1), :].rearrange("p n f -> p (n f)")

            def bias_parts(b, i):
                k = b * NT + i + 1
                dve.wait_ge(s_pk, k)
                v.tensor_reduce(MX[:, i % 2, 1, :], pPK[i % 2][:].rearrange("p (h m) -> p h m", m=M), AX_X,
                                ALU.max).then_inc(s_mxk, 1)
                dve.wait_ge(s_pq, k)
                v.tensor_reduce(MX[:, i % 2, 0, :], pPQ[:].rearrange("p (h m) -> p h m", m=M), AX_X,
                                ALU.max).then_inc(s_mxq, 1)
                dve.wait_ge(s_sq, k)
                v.tensor_reduce(SS[:, i % 2], SQ[:, i % 2, :].rearrange("p (a h k) -> p a h k", a=2, k=K), AX_X,
                                ALU.add).then_inc(s_ss, 1)
                dve.wait_ge(s_ss, k)
                dve.wait_ge(s_mxq, k)
                v.tensor_tensor(CC[:, i % 2], MX[:, i % 2], SS[:, i % 2], ALU.add).then_inc(s_cc, 1)
                dve.wait_ge(s_cc, k)
                if i >= 2:
                    dve.wait_ge(s_cT, k - 2)
                v.tensor_copy(CHL[:, i % 2, 0:2, 0, :], CC[:, i % 2]).then_inc(s_ch, 1)
                dve.wait_ge(s_ch, k)
                v.tensor_tensor(CHL[:, i % 2, 0:2, 1, :], CC[:, i % 2], CHL[:, i % 2, 0:2, 0, :].bitcast(F32),
                                ALU.subtract).then_inc(s_cl, 1)

            v.memset(held[:, 0:1], 0.0).then_inc(s_batch, 1)
            with dve.Fori(0, B) as b:
                dve.wait_ge(s_batch, b + 1)
                dve.wait_ge(s_x[0], b * 16 + 16)
                stats(b, 0, 0, row(X, b * GB))
                norm(b, 0, 0, tiles(XN[:, 0]), row(X, b * GB))
                lo_xn(b, 0)
                for i in range(NT):
                    g = i // T
                    bias_parts(b, i)
                    if g + 1 < GB:
                        if i % T == 0:
                            dve.wait_ge(s_x[g + 1], b * 16 + 16)
                            stats(b, 0, g + 1, row(X, b * GB + g + 1))
                        if i % T == 1:
                            norm(b, 0, g + 1, tiles(XN[:, g + 1]), row(X, b * GB + g + 1))
                        if i % T == 2:
                            lo_xn(b, g + 1)
                dve.wait_ge(s_kv, (b + 1) * NT)
                v.tensor_tensor(KVB[:].rearrange("p (c j k) -> p c j k", c=CH, j=HC),
                                pKV[:, 0:VW].rearrange("p (c j k) -> p c j k", c=CH, j=HC),
                                kvmask[:].unsqueeze(1).unsqueeze(3).to_broadcast([P, CH, HC, KE]),
                                ALU.mult).then_inc(s_kvall, 1)
                dve.wait_ge(s_ds, b + 1)
                v.tensor_copy(DS[:], pT[:, 0:VW]).then_inc(s_dsc, 1)
                dve.wait_ge(s_dsc, b + 1)

                def stage(g, k):
                    n = b * GB + g
                    if k == 0:
                        if g:
                            dve.wait_ge(s_aT, n)
                        for h in range(2):
                            m = 2 * n + h + 1
                            dve.wait_ge(s_num, m)
                            nb = NB[:, h].rearrange("p t h k -> p t (h k)")
                            v.tensor_tensor(nb, pF[h][:, 0:2 * VW].rearrange("p (t w) -> p t w", t=2),
                                            DS[:].unsqueeze(1).to_broadcast([P, 2, VW]), ALU.add).then_inc(s_nb, 1)
                            dve.wait_ge(s_nb, m)
                            v.reciprocal(RD[:, h], NB[:, h, :, :, K]).then_inc(s_rd, 1)
                            dve.wait_ge(s_rd, m)
                            v.tensor_tensor(AT[:, 2 * h:2 * h + 2], NB[:, h, :, :, 0:K],
                                            RD[:, h].unsqueeze(3).to_broadcast([P, 2, H, K]), ALU.mult).then_inc(s_at, 1)
                    if k == 2:
                        dve.wait_ge(s_wo, n + 1)
                        v.tensor_tensor(R1, pPQ[:], XN[:, g], ALU.add).then_inc(s_r1, 1)
                        hold(s_r1, n + 1)
                        stats(b, 1, g, R1)
                    if k == 3:
                        if g:
                            dve.wait_ge(s_nT, n)
                            dve.wait_ge(s_n1g, n)
                        norm(b, 1, g, tiles(N1), R1)
                    if k == 6:
                        dve.wait_ge(s_x2, n + 1)
                        dve.wait_ge(s_dn, n + 1)
                        v.tensor_tensor(R2, pQKV[:], X2, ALU.add).then_inc(s_r2, 1)
                        hold(s_r2, n + 1)
                        stats(b, 2, g, R2)
                    if k == 7:
                        if g:
                            dve.wait_ge(s_x1, n)
                        norm(b, 2, g, tiles(NY), R2)
                    if k == 8:
                        hold(s_y2, n + 1)
                        stats(b, 3, g, NY)
                    if k == 9:
                        norm(b, 3, g, tiles(NY), NY)
                    if k == 10:
                        hold(s_x1, n + 1)
                        stats(b, 4, g, row(X, n))
                    if k == 11:
                        dve.wait_ge(s_scat[g], (b + 1) * 16 * TOPK * T)
                        norm(b, 4, g, lambda t: PL[:, g, t, 0, 0:D], row(X, n))
                    if k == 12:
                        dve.wait_ge(s_xfh, n + 1)
                        v.tensor_tensor(row(XFL, n), pKV[:], row(XFH, n), ALU.subtract).then_inc(s_xfl, 1)
                    if k == 13:
                        dve.wait_ge(s_lg, n + 1)
                        v.tensor_copy(LG[:].rearrange("p t e -> p (t e)"), pKV[:, 0:T * E]).then_inc(s_lgc, 1)
                        hold(s_lgc, n + 1)
                        for t in range(T):
                            s = v.max(V8[:, t, :], LG[:, t, :])
                        s.then_inc(s_v8, 1)
                        hold(s_v8, n + 1)
                        for t in range(T):
                            s = v.max_index(I8[:, t, :], V8[:, t, :], LG[:, t, :])
                        s.then_inc(s_i8, 1)
                        v.tensor_tensor(GA[:], V8[:, :, 0], V8[:, :, 1], ALU.subtract).then_inc(s_gd, 1)
                        dve.wait_ge(s_i8, n + 1)
                        v.tensor_copy(I8f[:], I8[:, :, 0:TOPK]).then_inc(s_if, 1)
                        dve.wait_ge(s_if, n + 1)
                        for a in range(TOPK):
                            v.tensor_tensor(OH[:, a], iota8[:].unsqueeze(1).to_broadcast([P, T, E]),
                                            I8f[:, :, a:a + 1].to_broadcast([P, T, E]), ALU.is_equal).then_inc(s_oh, 1)
                        dve.wait_ge(s_oh, 2 * n + 2)
                        v.tensor_tensor(OHS[:], OH[:, 0], OH[:, 1], ALU.add).then_inc(s_ohs, 1)
                        v.tensor_copy(PL[:, g, :, :, ID_AT].bitcast(U32), IDS[:]).then_inc(s_pid, 1)
                        dve.wait_ge(s_pid, n + 1)
                        v.tensor_scalar(IDS[:], IDS[:], float(TOPK * GW), None, ALU.add).then_inc(s_ids, 1)
                        dve.wait_ge(s_ids, n + 1)
                    if k == 14:
                        dve.wait_ge(s_th, n + 1)
                        for a, sign in ((0, 0.5), (1, -0.5)):
                            v.tensor_scalar(PL[:, g, :, a, GATE_AT], TH[:], sign, 0.5, ALU.mult, ALU.add).then_inc(s_gt, 1)
                    if k == 15:
                        dve.wait_ge(s_rt, n + 1)
                        v.tensor_tensor(POS[:], pKV[:, 64:64 + T * E].rearrange("p (t e) -> p t e", e=E),
                                        BASE[:].unsqueeze(1).to_broadcast([P, T, E]), ALU.add).then_inc(s_pos, 1)
                        dve.wait_ge(s_pos, n + 1)
                        v.tensor_tensor(BASE[:], pKV[:, 128:128 + E], BASE[:], ALU.add).then_inc(s_base, 1)
                        v.tensor_tensor(OHP[:], OH[:], POS[:].unsqueeze(1).to_broadcast([P, TOPK, T, E]),
                                        ALU.mult).then_inc(s_ohp, 1)
                        dve.wait_ge(s_ohp, n + 1)
                        v.tensor_reduce(SLf[:].rearrange("p t a -> p a t"), OHP[:], AX_X, ALU.add).then_inc(s_slf, 1)
                        dve.wait_ge(s_slf, n + 1)
                        dve.wait_ge(s_gt, 2 * n + 2)
                        dve.wait_ge(s_base, n + 1)
                        v.tensor_copy(SLOT[:, g], SLf[:]).then_inc(s_slot, 1)

                pipeline(stage)
                dve.wait_ge(s_slot, (b + 1) * GB)
                dve.wait_ge(s_cpy, (b + 1) * GB)
                v.memset(held[:, 0:1], 0.0).then_inc(s_batch, 1)

            steps = [0]

            def step(ins):
                steps[0] += 1
                ins.then_inc(s_tab, 1)

            def settled():
                dve.wait_ge(s_tab, steps[0])

            step(v.tensor_copy(filslot[:], BASE[:]))
            step(v.tensor_tensor(CNT[:], BASE[:], ecap[:], ALU.subtract))
            settled()
            step(v.tensor_tensor(GTK, CNT[:].unsqueeze(2).to_broadcast([P, E, NK]),
                                 kb[:].unsqueeze(1).to_broadcast([P, E, NK]), ALU.is_gt))
            settled()
            step(v.tensor_reduce(NBK[:], GTK, AX_X, ALU.add))
            settled()
            step(v.tensor_tensor(CEM, leq[:], NBK[:].unsqueeze(1).to_broadcast([P, E, E]), ALU.mult))
            settled()
            step(v.tensor_reduce(CE[:], CEM, AX_X, ALU.add))
            settled()
            step(v.tensor_tensor(IND, jb[:].unsqueeze(2).to_broadcast([P, NBLK, E]),
                                 CE[:].unsqueeze(1).to_broadcast([P, NBLK, E]), ALU.is_ge))
            settled()
            step(v.tensor_reduce(EJ[:], IND, AX_X, ALU.add))
            step(v.tensor_tensor(INB, IND, NBK[:].unsqueeze(1).to_broadcast([P, NBLK, E]), ALU.mult))
            settled()
            step(v.tensor_reduce(CSJ[:], INB, AX_X, ALU.add))
            settled()
            v.tensor_tensor(RO[:], jb[:], CSJ[:], ALU.subtract).then_inc(s_pid, 1)
            dve.wait_ge(s_pid, NG + 1)
            v.tensor_scalar(ROWf[:], RO[:], float(BW), None, ALU.mult).then_inc(s_pid, 1)
            dve.wait_ge(s_pid, NG + 2)
            step(v.scalar_tensor_tensor(out=RO[:], in0=EJ[:], scalar=float(CAP), in1=ROWf[:], op0=ALU.mult, op1=ALU.add))
            settled()
            step(v.tensor_copy(ROW[:], RO[:]))
            step(v.tensor_scalar(EW[:], EJ[:], float(E - 1), 1.0, ALU.min, ALU.add))
            assert steps[0] == 13, steps

            def split(e, at, wait_e):
                dve.wait_ge(*wait_e)
                hi, lo = (b_[:, bass.ds(e, 1), :].rearrange("p e h -> p (e h)") for b_ in (E1H, E1L))
                v.tensor_scalar(hi, at, wscale[:], None, ALU.mult).then_inc(s_eh, 1)
                dve.wait_ge(s_eh, e + 1)
                v.scalar_tensor_tensor(out=lo, in0=at, scalar=wscale[:], in1=hi, op0=ALU.mult,
                                       op1=ALU.subtract).then_inc(s_el, 1)

            split(0, ST1[:, 0, :], (s_stage[0], 16))

            def shared(i):
                for q in range(2):
                    n = i * 2 + q
                    split(n + 1, ST1[:, (q + 1) % 2, :], (s_stage[(q + 1) % 2], i * 16 + (16 if q == 0 else 32)))
                    dve.wait_ge(s_sd, n + 1)
                    v.tensor_scalar(row(SH, n), (pQKV, pPQ)[q][:], 1.0, None, ALU.mult).then_inc(s_sh, 1)

            with dve.Fori(0, NG // 2) as i:
                shared(i)

            def lo_block(j, q):
                k = j * UNROLL + q
                dve.wait_ge(s_bh, k + 1)
                v.tensor_tensor(XBL[:, q % 2, :], (pT, pKV)[q % 2][:, 0:BW], XBH[:, q % 2, :],
                                ALU.subtract).then_inc(s_bl, 1)

            def result(j, q):
                wait(dve, s_ysc[q], j * 32)
                dve.wait_ge(s_do, j * UNROLL + q + 1)
                for t in range(2):
                    s = v.tensor_scalar(Y[q][:, t, :], (pQKV, pPQ)[q % 2][:, t * P:(t + 1) * P],
                                        XS[q][:, t, GATE_AT:GATE_AT + 1], None, ALU.mult)
                s.then_inc(s_y, 1)

            def blocks(j, last):
                for q in range(UNROLL):
                    if q + 1 < UNROLL:
                        lo_block(j, q + 1)
                    elif not last:
                        lo_block(j + 1, 0)
                    if q:
                        result(j, q - 1)
                    elif not isinstance(j, int) or j:
                        result(j - 1, UNROLL - 1)

            lo_block(0, 0)
            blocks(0, False)
            with dve.Fori(1, NBLK // UNROLL - 1) as j:
                blocks(j, False)
            blocks(NBLK // UNROLL - 1, True)
            result(NBLK // UNROLL - 1, UNROLL - 1)

            def finish(i):
                for q in range(2):
                    n = i * 2 + q
                    dve.wait_ge(s_ya, n + 1)
                    v.tensor_tensor(ACC[q], row(SH, n), AY[q], ALU.add).then_inc(s_acc, 1)
                    hold(s_acc, n + 1)
                    for t in range(T):
                        s = v.bn_stats(st5[:, q, t, :], ACC[q][:, t * D:(t + 1) * D])
                    s.then_inc(s_bn5, 1)
                    hold(s_bn5, n + 1)
                    for t in range(T):
                        s = v.bn_aggr(mv5[:, q, t, :], st5[:, q, t, :])
                    s.then_inc(s_mv5, 1)
                for q in range(2):
                    n = i * 2 + q
                    dve.wait_ge(s_rs5, n + 1)
                    for t in range(T):
                        s = v.tensor_scalar(N5[q][:, t * D:(t + 1) * D], ACC[q][:, t * D:(t + 1) * D],
                                            mv5[:, q, t, 0:1], rs5[:, q, t:t + 1], ALU.subtract, ALU.mult)
                    s.then_inc(s_no5, 1)
                    wait(dve, s_st[q], i * 16)
                    dve.wait_ge(s_no5, n + 1)
                    v.tensor_tensor(OUT[q], row(X, n), N5[q], ALU.add).then_inc(s_out, 1)

            finish(0)
            with dve.Fori(1, NG // 2) as i:
                finish(i)


_OUTS = [((B, S, D), 'float32')]


def kernel(**inputs):
    import numpy as np
    import concourse.bacc as bacc
    from concourse import mybir as mb
    from concourse.bass_utils import run_bass_kernel_spmd as run

    f = lambda n: np.asarray(inputs[n])
    wq, wk, wv = (f(f"L0_attn_{n}").reshape(D, H * K) for n in ("wq", "wk", "wv"))
    arrays = {
        "x": f("L0_attn_x"),
        "wqkv": np.concatenate([wq, wk, wv], axis=1),
        "wqkT": np.stack([wq.T, wk.T], axis=1),
        "omT": np.tile(f("L0_attn_omega").T, (H, 1)),
        "wo": f("L0_attn_wo"),
        "cols": np.concatenate([f("L0_attn_ln1_g")[:, None], f("L0_attn_ln1_b")[:, None],
                                f("L0_attn_b1").reshape(FC, P).T], axis=1),
        "rows": np.concatenate([f(f"L0_attn_{n}") for n in ("ln1_g", "ln1_b", "b2", "ln2_g", "ln2_b")])[None, :],
        "w1": f("L0_attn_w1"),
        "w2": f("L0_attn_w2").reshape(FC, P, D).transpose(1, 0, 2),
        "ew1T": np.concatenate([f("L0_ffn_shared_w1")[None], f("L0_ffn_experts_w1")]).transpose(2, 0, 1),
        "ew2T": np.concatenate([f("L0_ffn_shared_w2")[None], f("L0_ffn_experts_w2")])
                  .reshape(E + 1, D, EC, P).transpose(3, 0, 2, 1),
        "gwT": f("L0_ffn_gate_w").T,
    }
    nc = bacc.Bacc("TRN2", target_bir_lowering=False, num_devices=1)
    feed, args = {}, []
    for name, a in arrays.items():
        a = np.ascontiguousarray(a)
        feed[f"in_{name}"] = a
        args.append(nc.dram_tensor(f"in_{name}", a.shape, mb.dt.from_np(a.dtype), kind="ExternalInput").ap())
    for i, (shape, dtype) in enumerate(_OUTS):
        args.append(nc.dram_tensor(f"out_{i}", shape, mb.dt.from_np(np.dtype(dtype)), kind="ExternalOutput").ap())
    xs = nc.dram_tensor("xs", (XROWS, RW), mb.dt.float32).ap()
    ys = nc.dram_tensor("ys", (YROWS, D), mb.dt.float32).ap()
    build(nc, xs, ys, *args)
    r = run(nc, [feed], core_ids=[0])
    return r.results[0]["out_0"]
```

```python
from contextlib import ExitStack

import concourse.bass as bass
from concourse import mybir

F32 = mybir.dt.float32
F32R = mybir.dt.float32r
F16 = mybir.dt.float16
BF16 = mybir.dt.bfloat16
I32 = mybir.dt.int32
U32 = mybir.dt.uint32
ALU = mybir.AluOpType
ACT = mybir.ActivationFunctionType
AX_X = mybir.AxisListType.X

P = 128
D = 128
B, S = 2, 2048
T = 4
GW = T * P
GB = S // GW
NG = B * GB
NT = GB * T
H, K, M = 16, 8, 32
HM = H * M
CH = HM // P
HC = H // CH
KE = K + 1
VW = H * KE
FF = 512
FC = FF // P
E = 8
HID = 512
EC = HID // P
SCALE = float(K) ** -0.25
DELTA = 1e-6 * float(M) ** 0.5
EPS_IN, EPS_OUT = 1e-5, 1e-6
LN_EPS = [EPS_IN, EPS_OUT, EPS_OUT, EPS_IN, EPS_IN]

TOPK = 2
BW = 2 * P
UNROLL = 8
NBLK = -(-(TOPK * B * S // BW + E - 1) // UNROLL) * UNROLL
CAP = B * S + BW
RESULTS = TOPK * B * S
SPARE = NBLK * BW - RESULTS
XROWS = E * CAP + SPARE
YROWS = RESULTS + E * BW + SPARE
RW = D + 4
GATE_AT, ID_AT = D, D + 1
assert SPARE == E * BW and E // B <= FC and HID == GW


def build(nc, xs, ys, sh, x, wqkv, wqkT, omT, wo, cols, rows, w1, w2, ew1T, ew2T, gwT, out):
    x_v = x.rearrange("b (g p t) d -> (b g) p (t d)", p=P, t=T)
    out_v = out.rearrange("b (g p t) d -> (b g) p (t d)", p=P, t=T)
    ys_v = ys[0:RESULTS].rearrange("(n p c) d -> n p (c d)", p=P, c=T * TOPK)

    with ExitStack() as ctx:
        def sb(name, shape, dt=F32):
            return ctx.enter_context(nc.sbuf_tensor(name, shape, dt))

        def psum(name):
            return ctx.enter_context(nc.psum_tensor(name, [P, 512], F32))

        def sem(name):
            return ctx.enter_context(nc.semaphore(name))

        X = sb("X", [P, NG, GW])
        XN = sb("XN", [P, GB, GW])
        XTH = sb("XTH", [P, 2, GW], F32R)
        XTL = sb("XTL", [P, 2, GW], F32R)
        WA = H * K * 3 + 2 * HM
        WH = sb("WH", [P, WA], F32R)
        WL = sb("WL", [P, WA], F32R)
        wo_s = sb("wo_s", [P, P])
        cols_s = sb("cols_s", [P, 2 + FC])
        rows_s = sb("rows_s", [P, 5, P])
        b12 = sb("b12", [P, P])
        w1_s = sb("w1_s", [P, FF])
        w2_s = sb("w2_s", [P, FC, P])
        gwT_s = sb("gwT_s", [P, E])
        ident = sb("ident", [P, P])
        headmask = sb("headmask", [P, H])
        kvmask = sb("kvmask", [P, HC])
        selQ = sb("selQ", [64, HM], F32R)
        selK = sb("selK", [64, HM], F32R)
        delta = sb("delta", [P, P])
        zeros = sb("zeros", [P, T])
        halves = sb("halves", [P, T])
        eps = sb("eps", [P, 2, T])
        held = sb("held", [P, 6 + GB])
        st = sb("st", [P, 5, GB, T, 6])
        mv = sb("mv", [P, 5, GB, T, 2])
        ve = sb("ve", [P, 5, GB, T])
        rs = sb("rs", [P, 5, GB, T])
        SQ = sb("SQ", [P, 2, 2 * D])
        XFT = SQ[:].rearrange("p a d -> p (a d)")
        VX = sb("VX", [P, 3, H, KE])
        MX = sb("MX", [P, 2, 2, H])
        SS = sb("SS", [P, 2, 2, H])
        CC = sb("CC", [P, 2, 2, H])
        CHL = sb("CHL", [P, 2, 4, 2, H], F32R)
        CT = sb("CT", [64, 2, GW], F32R)
        PK = sb("PK", [P, 2, HM])
        PQT = sb("PQT", [P, GB, CH, GW])
        KVB = sb("KVB", [P, VW])
        DS = sb("DS", [P, VW])
        NB = sb("NB", [P, 2, 2, H, KE])
        RD = sb("RD", [P, 2, 2, H])
        AT = sb("AT", [P, T, H, K])
        ATX = sb("ATX", [P, 2, GW])
        ATT, X1T = ATX[:, 0, :], ATX[:, 1, :]
        MID = sb("MID", [P, 5, GW])
        R1, N1, R2 = (MID[:, i, :] for i in range(3))
        NY = [MID[:, 3, :], MID[:, 4, :]]
        HT = sb("HT", [P, FC, GW])
        XFH = sb("XFH", [P, NG, GW], F16)
        XFL = sb("XFL", [P, NG, GW], F16)
        iota8 = sb("iota8", [P, E])
        LG = sb("LG", [P, T, E])
        V8 = sb("V8", [P, T, 8])
        I8 = sb("I8", [P, T, 8], U32)
        I8f = sb("I8f", [P, T, TOPK])
        GA = sb("GA", [P, T])
        TH = sb("TH", [P, T])
        OH = sb("OH", [P, TOPK, T, E])
        OHS = sb("OHS", [P, T, E], BF16)
        POS = sb("POS", [P, T, E])
        OHP = sb("OHP", [P, TOPK, T, E])
        SLf = sb("SLf", [P, T, TOPK])
        SLOT = sb("SLOT", [P, GB, T, TOPK], U32)
        BASE = sb("BASE", [P, E])
        IDS = sb("IDS", [P, T, TOPK])
        PL = sb("PL", [P, GB, T, TOPK, RW])
        before = sb("before", [P, P], BF16)
        ones_b = sb("ones_b", [P, P], BF16)
        filslot = sb("filslot", [P, E], U32)
        ecap = sb("ecap", [P, E])
        leq = sb("leq", [P, E, E])
        NK = B * S // BW
        kb = sb("kb", [P, NK])
        CNT = sb("CNT", [P, E])
        NBK = sb("NBK", [P, E])
        CE = sb("CE", [P, E])
        jb = sb("jb", [P, NBLK])
        IND, INB = (HT[:, i, 0:NBLK * E].rearrange("p (j e) -> p j e", e=E) for i in range(2))
        GTK = HT[:, 2, 0:E * NK].rearrange("p (e k) -> p e k", e=E)
        CEM = HT[:, 3, 0:E * E].rearrange("p (a e) -> p a e", a=E)
        EJ = sb("EJ", [P, NBLK])
        CSJ = sb("CSJ", [P, NBLK])
        RO = sb("RO", [P, NBLK])
        ROWf = sb("ROWf", [P, NBLK])
        ROW = sb("ROW", [P, NBLK], U32)
        EW = sb("EW", [P, NBLK], U32)
        ssum = sb("ssum", [P, 1])
        stot = sb("stot", [P, 1])
        hexp = sb("hexp", [P, 1], U32)
        wscale = sb("wscale", [P, 1])
        wunscale = sb("wunscale", [P, 1])
        E1H = sb("E1H", [P, E + 1, HID], F16)
        E1L = sb("E1L", [P, E + 1, HID], F16)
        E2 = sb("E2", [P, E + 1, EC, D])
        XBH, XBL = (PK[:, i, :].bitcast(F16)[:, 0:2 * BW].rearrange("p (q s) -> p q s", q=2) for i in range(2))
        st5 = sb("st5", [P, 2, T, 6])
        mv5 = sb("mv5", [P, 2, T, 2])
        ve5 = sb("ve5", [P, 2, T])
        rs5 = sb("rs5", [P, 2, T])
        mm5 = sb("mm5", [P, 2, T])
        nm5 = sb("nm5", [P, 2, T])

        pq = PQT[:].rearrange("p g c f -> p (g c f)")

        def parts(flat, *widths):
            at = 0
            for w in widths:
                yield flat[:, at:at + w]
                at += w

        EW1, W_f, wqkT_f, omT_s, omBD_f, ones, sel_a, sel_b = parts(
            pq, (E + 1) * HID, 3 * D, 2 * P, M, HM, HM, HM, HM)
        wqkT_s = wqkT_f.rearrange("p (i d) -> p i d", i=2)
        omBD = omBD_f.rearrange("p (h m) -> p h m", h=H)
        XS = [v.rearrange("p (t w) -> p t w", t=2) for v in parts(pq, *[2 * RW] * UNROLL)]
        mid = MID[:].rearrange("p a f -> p (a f)")
        Y = [v.rearrange("p (t d) -> p t d", t=2) for v in parts(mid, *[2 * D] * UNROLL)]
        SPR = mid[:, 0:E * 2 * RW].rearrange("p (c w) -> p c w", w=RW)
        FIL = pq[:, UNROLL * 2 * RW:(UNROLL + E) * 2 * RW].rearrange("p (e a w) -> p e a w", e=E, a=2)
        YC = [mid[:, 0:2 * GW], mid[:, 2 * GW:4 * GW]]
        W1S = HT
        SH = [PK[:, q, :] for q in range(2)]
        AY = [HT[:, 0, :], HT[:, 1, :]]
        ACC = [HT[:, 2, :], HT[:, 3, :]]
        N5 = [XN[:, 0, :], XN[:, 1, :]]
        OUT = [XN[:, 2, :], XN[:, 3, :]]

        pT, pQKV, pPQ = psum("pT"), psum("pQKV"), psum("pPQ")
        pPK = [psum("pPK0"), psum("pPK1")]
        pF = [psum("pF0"), psum("pF1")]
        pKV = psum("pKV")

        s_x = [sem(f"x_loaded{g}") for g in range(GB)]
        s_w, s_ew1, s_w2 = sem("weights_loaded"), sem("expert_w1_loaded"), sem("expert_w2_loaded")
        s_stage = [sem(f"staged{i}") for i in range(E // B)]
        s_const, s_prep_p, s_prep_v = sem("pool_constants"), sem("prep_products"), sem("prep_by_dve")
        s_batch = sem("batch_done")
        s_bn, s_mv, s_rs, s_no = ([sem(f"{n}{j}") for j in range(5)] for n in (
            "bn_stats", "mean_var", "rstd", "normed"))
        s_ve = sem("var_eps")
        s_shst = [sem(f"shared_stored{q}") for q in range(2)]
        s_xT, s_xh, s_xl = sem("xn_turned"), sem("xn_hi"), sem("xn_lo")
        s_qkv, s_pk, s_pq = sem("qkv_ready"), sem("pk_raw"), sem("pq_raw")
        s_sq, s_vx = sem("squares"), sem("v_copied")
        s_mxk, s_mxq, s_ss, s_cc, s_ch, s_cl = (sem(n) for n in (
            "max_k", "max_q", "sq_sum", "c_sum", "c_hi", "c_lo"))
        s_cT, s_ct, s_pkb, s_ek = sem("c_turned"), sem("c_copied"), sem("pk_biased"), sem("exp_k")
        s_kv, s_kvall, s_fm, s_eq = sem("kv_step"), sem("kv_masked"), sem("pq_biased"), sem("exp_q")
        s_ds, s_dsc = sem("dsum"), sem("dsum_copied")
        s_num, s_nb, s_rd, s_at = sem("num_den"), sem("num_den_copied"), sem("den_recip"), sem("attn")
        s_aT, s_att, s_wo, s_r1 = sem("attn_turned"), sem("attn_copied"), sem("wo_done"), sem("res1")
        s_nT, s_x1t, s_up, s_ge, s_dn, s_r2 = (sem(n) for n in (
            "n1_turned", "x1t", "up_done", "gelu_done", "down_done", "res2"))
        s_n2g, s_y2, s_x1 = sem("n2_times_g"), sem("y_ready"), sem("x1_ready")
        s_fT, s_xft, s_xfh, s_xfl, s_lg, s_lgc = (sem(n) for n in (
            "xf_turned", "xf_copied", "xf_hi", "xf_lo", "logits", "logits_copied"))
        s_v8, s_i8, s_if, s_gd, s_th, s_gt, s_oh, s_ohs = (sem(n) for n in (
            "top8", "top8_index", "index_float", "top2_gap", "tanh_gap", "gates", "onehots", "onehot_sum"))
        s_pid, s_ids, s_cpy = sem("row_ids"), sem("ids_next"), sem("row_copied")
        s_rt, s_pos, s_base, s_ohp, s_slf, s_slot = (sem(n) for n in (
            "routed", "positions", "base_next", "slot_terms", "slot_float", "slots"))
        s_scat = [sem(f"scattered{g}") for g in range(GB)]
        s_n1g, s_x2 = sem("n1_times_g"), sem("x2_ready")
        s_free, s_spare = sem("rows_sent"), sem("spare_written")
        s_tab, s_fil, s_fill = sem("table_step"), sem("filler_rows_step"), sem("fillers_written")
        s_ssq, s_sc = sem("w1_squares_summed"), sem("scale_step")
        s_eh, s_el = sem("w1_hi"), sem("w1_lo")
        s_su, s_ss1, s_sd, s_sh = sem("shared_up"), sem("shared_silu"), sem("shared_down"), sem("shared_copied")
        s_bx = [sem(f"block_loaded{q}") for q in range(UNROLL)]
        s_bT, s_bh, s_bl, s_u, s_si, s_do, s_y = (sem(n) for n in (
            "block_turned", "block_hi", "block_lo", "block_up", "block_silu", "block_down", "block_result"))
        s_take = sem("result_taken")
        s_ysc = [sem(f"result_scattered{q}") for q in range(UNROLL)]
        s_yc = [sem(f"results_loaded{q}") for q in range(2)]
        s_ya, s_acc, s_bn5, s_mv5, s_ve5, s_nm5, s_no5, s_out = (sem(n) for n in (
            "routed_sum", "all_sum", "bn5", "mv5", "root_step5", "mean_rstd5", "no5", "out_ready"))
        s_st = [sem(f"stored{q}") for q in range(2)]

        NLOADS = 9
        NCONST = 32
        NPREP = 13

        def wait(eng, s, value):
            if not isinstance(value, int) or value > 0:
                eng.wait_ge(s, value)

        def tiles(buf):
            return lambda t: buf[:, t * D:(t + 1) * D]

        def row(buf, n):
            return buf[:, bass.ds(n, 1), :].rearrange("p n f -> p (n f)")

        STAGGER, STAGES = 2, 21

        def pipeline(stage):
            for step in range(STAGGER * (GB - 1) + STAGES):
                for g in range(GB):
                    if 0 <= step - STAGGER * g < STAGES:
                        stage(g, step - STAGGER * g)

        block = ctx.enter_context(nc.Block())

        @block.sync
        def _(sp):
            sp.dma_start(X[:, 0, :], x_v[0]).then_inc(s_x[0], 16)
            sp.dma_start(wqkT_s, wqkT).then_inc(s_w, 16)
            sp.dma_start(omT_s, omT).then_inc(s_w, 16)
            sp.dma_start(W_f, wqkv).then_inc(s_w, 16)
            sp.dma_start(rows_s[:].rearrange("p v d -> p (v d)"), rows.to_broadcast([P, 5 * P])).then_inc(s_w, 16)
            sp.dma_start(cols_s[:], cols).then_inc(s_w, 16)
            sp.dma_start(gwT_s[:], gwT).then_inc(s_w, 16)
            sp.dma_start(wo_s[:], wo).then_inc(s_w, 16)
            sp.dma_start(w1_s[:], w1).then_inc(s_w, 16)
            sp.dma_start(w2_s[:], w2).then_inc(s_w, 16)
            sp.dma_start(EW1.rearrange("p (e h) -> p e h", e=E + 1), ew1T).then_inc(s_ew1, 16)
            for g in range(1, GB):
                sp.dma_start(X[:, g, :], x_v[g]).then_inc(s_x[g], 16)
            for g in range(GB):
                sp.wait_ge(s_x[g], 16)
                sp.dma_start(X[:, GB + g, :], x_v[GB + g]).then_inc(s_x[g], 16)
            sp.dma_start(E2[:], ew2T).then_inc(s_w2, 16)
            sp.wait_ge(s_fil, 2)
            for g in range(GB):
                n = SPARE // GB
                sp.dma_start(xs[E * CAP + g * n:E * CAP + (g + 1) * n].rearrange("(p a) w -> p a w", p=P),
                             SPR[:, g * n // P:(g + 1) * n // P]).then_inc(s_spare, 16)
            with sp.Fori(0, B) as b:
                sp.wait_ge(s_batch, b + 1)
                for m in range(E // B):
                    w = ew1T[:, bass.ds(b * (E // B) + m + 1, 1), :].rearrange("p e h -> p (e h)")
                    sp.dma_start(W1S[:, m, :], w).then_inc(s_stage[m], 16)
                for g in range(GB):
                    sp.wait_ge(s_sh, b * GB + g + 1)
                    sp.dma_start(sh[bass.ds(b * GB + g, 1)].rearrange("n p f -> (n p) f"),
                                 SH[g % 2]).then_inc(s_shst[g % 2], 16)
            sp.wait_ge(s_fil, 4)
            sp.wait_ge(s_tab, 2)
            for e in range(E):
                row = sp.value_load(filslot[0:1, e:e + 1], min_val=0, max_val=XROWS - BW)
                sp.dma_start(xs[bass.ds(row, BW)].rearrange("(p a) w -> p a w", a=2), FIL[:, e]).then_inc(s_fill, 16)
            sp.wait_ge(s_fill, 16 * E)
            for g in range(GB):
                sp.wait_ge(s_scat[g], 16 * TOPK * T * B)
            sp.wait_ge(s_tab, 13)

            def load_blocks(j):
                for q in range(UNROLL):
                    row = sp.value_load(ROW[0:1, bass.ds(j * UNROLL + q, 1)], min_val=0, max_val=XROWS - BW)
                    wait(sp, s_ysc[q], j * 32)
                    sp.dma_start(XS[q], xs[bass.ds(row, BW)].rearrange("(p a) w -> p a w", a=2)).then_inc(s_bx[q], 16)

            load_blocks(0)
            with sp.Fori(1, NBLK // UNROLL) as j:
                load_blocks(j)
            for q in range(UNROLL):
                sp.wait_ge(s_ysc[q], 32 * (NBLK // UNROLL))

            def load_results(i):
                for q in range(2):
                    wait(sp, s_ya, i * 2 + q - 1)
                    sp.dma_start(YC[q], ys_v[bass.ds(i * 2 + q, 1)].rearrange("n p f -> (n p) f")).then_inc(s_yc[q], 16)
                    wait(sp, s_acc, i * 2 + q - 1)
                    sp.dma_start(SH[q], sh[bass.ds(i * 2 + q, 1)].rearrange("n p f -> (n p) f")).then_inc(s_shst[q], 16)

            load_results(0)
            with sp.Fori(1, NG // 2) as i:
                load_results(i)

        @block.gpsimd
        def _(pool):
            eng = nc.gpsimd
            count = [0]

            def const(ins):
                count[0] += 1
                ins.then_inc(s_const, 1)

            def settle():
                pool.wait_ge(s_const, count[0])

            const(eng.memset(ones, 1.0))
            const(eng.memset(sel_a, -1.0))
            const(eng.memset(eps[:, 0, :], EPS_IN))
            const(eng.memset(eps[:, 1, :], EPS_OUT))
            const(eng.memset(zeros[:], 0.0))
            const(eng.memset(halves[:], -0.5))
            settle()
            const(eng.affine_select(out=ident[:], in_=ones[:, 0:P], compare_op=ALU.is_equal, fill=0.0, base=0,
                                    pattern=[[-1, P]], channel_multiplier=1))
            const(eng.affine_select(out=headmask[:], in_=ones[:, 0:H], compare_op=ALU.is_ge, fill=0.0, base=0,
                                    pattern=[[-K, H]], channel_multiplier=1))
            const(eng.affine_select(out=kvmask[:], in_=ones[:, 0:HC], compare_op=ALU.is_ge, fill=0.0, base=0,
                                    pattern=[[-M, HC]], channel_multiplier=1))
            settle()
            const(eng.affine_select(out=headmask[:], in_=headmask[:], compare_op=ALU.is_ge, fill=0.0, base=K - 1,
                                    pattern=[[K, H]], channel_multiplier=-1))
            const(eng.affine_select(out=kvmask[:], in_=kvmask[:], compare_op=ALU.is_ge, fill=0.0, base=M - 1,
                                    pattern=[[M, HC]], channel_multiplier=-1))
            def selector(dst, offset):
                const(eng.affine_select(out=dst[0:64].rearrange("p (h m) -> p h m", m=M),
                                        in_=sel_a[0:64].rearrange("p (h m) -> p h m", m=M),
                                        compare_op=ALU.is_equal, fill=0.0, base=-offset,
                                        pattern=[[-1, H], [0, M]], channel_multiplier=1))

            sel4 = [HT[:, i, :] for i in range(4)]
            for i in range(4):
                selector(sel4[i], i * H)
            settle()
            const(eng.tensor_tensor(sel_b[0:64], sel4[0][0:64], sel4[1][0:64], ALU.add))
            const(eng.tensor_tensor(MID[0:64, 0, :], sel4[2][0:64], sel4[3][0:64], ALU.add))
            const(eng.memset(delta[:], DELTA))
            const(eng.memset(VX[:], 1.0))
            settle()
            ints = HT[:, 0, 0:E + E + NK + NBLK].bitcast(I32)
            i8, iec, ikb, ijb = parts(ints, E, E, NK, NBLK)
            ids = HT[:, 1, 0:T * TOPK].bitcast(I32)
            const(eng.iota(i8, pattern=[[1, E]], base=0, channel_multiplier=0))
            const(eng.iota(iec, pattern=[[CAP, E]], base=0, channel_multiplier=0))
            const(eng.iota(ikb, pattern=[[BW, NK]], base=0, channel_multiplier=0))
            const(eng.iota(ijb, pattern=[[1, NBLK]], base=0, channel_multiplier=0))
            const(eng.iota(ids, pattern=[[TOPK, T], [1, TOPK]], base=0, channel_multiplier=T * TOPK))
            const(eng.memset(ones_b[:], 1.0))
            settle()
            for dst, i in ((iota8, i8), (ecap, iec), (kb, ikb), (jb, ijb)):
                const(eng.tensor_copy(dst[:], i))
            const(eng.tensor_copy(IDS[:].rearrange("p t a -> p (t a)"), ids))
            const(eng.affine_select(out=before[:], in_=ones_b[:], compare_op=ALU.is_gt, fill=0.0, base=0,
                                    pattern=[[1, P]], channel_multiplier=-1))
            const(eng.affine_select(out=leq[:], in_=ones[:, 0:E * E].rearrange("p (a b) -> p a b", a=E),
                                    compare_op=ALU.is_ge, fill=0.0, base=0, pattern=[[1, E], [-1, E]],
                                    channel_multiplier=0))
            assert count[0] == NCONST, count
            eng.memset(PL[:], 0.0).then_inc(s_free, 1)
            pool.wait_ge(s_w, 16 * NLOADS)
            eng.tensor_tensor(b12[:], rows_s[:, 1, :], rows_s[:, 2, :], ALU.add).then_inc(s_const, 1)
            pool.wait_ge(s_const, NCONST + 1)
            pool.wait_ge(s_ssq, 1)
            eng.partition_all_reduce(stot[:], ssum[:], P, bass.bass_isa.ReduceOp.add).then_inc(s_ssq, 1)

            def hold(s, value, at=1):
                pool.wait_ge(s, value)
                return eng.tensor_tensor(held[:, at:at + 1], halves[:, 0:1], halves[:, 1:2], ALU.add)

            roots = [0]

            def rstd(b, j, g):
                pool.wait_ge(s_mv[j], b * GB + g + 1)
                eng.tensor_tensor(ve[:, j, g, :], mv[:, j, g, :, 1], eps[:, int(LN_EPS[j] == EPS_OUT), :],
                                  ALU.add).then_inc(s_ve, 1)
                if j:
                    roots[0] += 1
                pool.wait_ge(s_ve, b * (5 * GB) + (GB + roots[0] if j else g + 1))
                eng.tensor_tensor(rs[:, j, g, :], ve[:, j, g, :], halves[:], ALU.pow).then_inc(s_rs[j], 1)

            def affine(b, g, s_in, src, dst, gain, bias, s_mid, s_end):
                pool.wait_ge(s_in, b * GB + g + 1)
                d, n = (v.rearrange("p (t d) -> p t d", t=T) for v in (dst, src))
                eng.tensor_tensor(d, n, gain.unsqueeze(1).to_broadcast([P, T, D]), ALU.mult).then_inc(s_mid, 1)
                pool.wait_ge(s_mid, b * GB + g + 1)
                eng.tensor_tensor(d, d, bias.unsqueeze(1).to_broadcast([P, T, D]), ALU.add).then_inc(s_end, 1)

            def scatter_rows(g):
                for t in range(T):
                    for a in range(TOPK):
                        eng.indirect_dma_start(xs, bass.IndirectOffsetOnAxis(SLOT[:, g, t, a:a + 1], 0),
                                               PL[:, g, t, a, :], None).then_inc(s_scat[g], 16)

            pool.wait_ge(s_prep_v, NPREP)

            def zero_rows(buf, step, pattern, base, per_partition):
                eng.memset(buf, 0.0).then_inc(s_fil, 1)
                pool.wait_ge(s_fil, step)
                eng.iota(buf.bitcast(I32)[..., ID_AT], pattern=pattern, base=base,
                         channel_multiplier=per_partition).then_inc(s_fil, 1)

            n = SPARE // GB
            zero_rows(SPR, 1, [[n, GB], [1, n // P]], RESULTS + E * BW, n // P)
            def send_rows(b, g):
                pool.wait_ge(s_cpy, b * GB + g + 1)
                hold(s_slot, b * GB + g + 1, at=5 + g)
                scatter_rows(g)

            def attend(b, last):
                roots[0] = 0

                def stage(g, k):
                    n = b * GB + g
                    if k == 20 and g < (GB - 1 if last else 1):
                        send_rows(b, g)
                    if k == 4:
                        rstd(b, 1, g)
                    if k == 9:
                        rstd(b, 2, g)
                    if k == 10:
                        affine(b, g, s_no[2], NY[g % 2], NY[g % 2], rows_s[:, 3, :], rows_s[:, 4, :], s_n2g, s_y2)
                    if k == 11:
                        rstd(b, 3, g)
                    if k == 12:
                        xg = X[:, bass.ds(n, 1), :].rearrange("p n f -> p (n f)")
                        pool.wait_ge(s_no[3], n + 1)
                        eng.tensor_tensor(xg, xg, NY[g % 2], ALU.add).then_inc(s_x1, 1)
                    if k == 13 and g == GB - 1 and last:
                        pool.wait_ge(s_num, 2 * NG)
                        zero_rows(FIL, 3, [[BW, E], [1, 2]], RESULTS, 2)
                    if k == 13:
                        rstd(b, 4, g)

                pipeline(stage)

            for g in range(GB):
                rstd(0, 0, g)
            with pool.Fori(0, B - 1) as b:
                attend(b, False)
                for g in range(GB):
                    rstd(b + 1, 0, g)
                    if g + 1 < GB:
                        send_rows(b, g + 1)
                for g in range(GB):
                    pool.wait_ge(s_scat[g], (b + 1) * (16 * TOPK * T))
                eng.tensor_tensor(held[:, 5 + GB:6 + GB], halves[:, 0:1], halves[:, 1:2], ALU.add).then_inc(s_free, 1)
            attend(B - 1, True)
            send_rows(B - 1, GB - 1)

            def scatter_results(j):
                for q in range(UNROLL):
                    pool.wait_ge(s_take, j * UNROLL + q + 1)
                    hold(s_y, j * UNROLL + q + 1, at=2).then_inc(s_take, 1)
                    for t in range(2):
                        eng.indirect_dma_start(ys, bass.IndirectOffsetOnAxis(XS[q][:, t, ID_AT:ID_AT + 1].bitcast(U32), 0),
                                               Y[q][:, t, :], None).then_inc(s_ysc[q], 16)

            eng.memset(held[:, 2:3], 0.0).then_inc(s_take, 1)
            with pool.Fori(0, NBLK // UNROLL) as j:
                scatter_results(j)

            def add_routed(i, q):
                pool.wait_ge(s_yc[q], i * 16 + 16)
                y = YC[q].rearrange("p (t a d) -> p t a d", t=T, a=TOPK)
                eng.tensor_tensor(AY[q].rearrange("p (t d) -> p t d", t=T), y[:, :, 0], y[:, :, 1],
                                  ALU.add).then_inc(s_ya, 1)

            def root5(i, q):
                n = i * 2 + q
                pool.wait_ge(s_mv5, n + 1)
                eng.tensor_tensor(mm5[:, q], zeros[:], mv5[:, q, :, 0], ALU.subtract)
                eng.tensor_tensor(ve5[:, q], mv5[:, q, :, 1], eps[:, 0, :], ALU.add).then_inc(s_ve5, 1)
                pool.wait_ge(s_ve5, 2 * n + 1)
                eng.tensor_tensor(rs5[:, q], ve5[:, q], halves[:], ALU.pow).then_inc(s_ve5, 1)
                pool.wait_ge(s_ve5, 2 * n + 2)
                eng.tensor_tensor(nm5[:, q], mm5[:, q], rs5[:, q], ALU.mult).then_inc(s_nm5, 1)

            for q in range(2):
                add_routed(0, q)
            with pool.Fori(0, NG // 2 - 1) as i:
                for q in range(2):
                    root5(i, q)
                    add_routed(i + 1, q)
            for q in range(2):
                root5(NG // 2 - 1, q)

        @block.tensor
        def _(pe):
            def three(o, a, b_, stop=True):
                nc.tensor.matmul(o, a[0], b_[0], start=True, stop=False)
                nc.tensor.matmul(o, a[0], b_[1], start=False, stop=False)
                return nc.tensor.matmul(o, a[1], b_[0], start=False, stop=stop)

            def turn(bank, src):
                for t in range(T):
                    m = nc.tensor.transpose(bank[:, t * P:(t + 1) * P], src(t), ident[:])
                return m

            pe.wait_ge(s_prep_v, 2)
            for i in range(2):
                nc.tensor.matmul(pF[i][:], wqkT_s[:, i, :], omBD_f, start=True, stop=True).then_inc(s_prep_p, 1)
            pe.wait_ge(s_prep_v, NPREP)

            def turn_xn(b, g):
                pe.wait_ge(s_no[0], b * GB + g + 1)
                turn(pT, lambda t: XN[:, g, t * P:(t + 1) * P]).then_inc(s_xT, 1)

            w = lambda a, n: [v[:, a:a + n] for v in (WH, WL)]

            def xt(i):
                return [v[:, i // T % 2, i % T * P:(i % T + 1) * P] for v in (XTH, XTL)]

            def qkv_pk(b, i):
                if i % T == 0:
                    pe.wait_ge(s_xl, b * GB + i // T + 1)
                if i:
                    pe.wait_ge(s_vx, b * NT + i)
                three(pQKV[:, 0:3 * D], xt(i), w(0, 3 * D)).then_inc(s_qkv, 1)
                if i >= 2:
                    pe.wait_ge(s_ek, b * NT + i - 1)
                three(pPK[i % 2][:], xt(i), w(3 * D + HM, HM)).then_inc(s_pk, 1)

            def pq(b, i):
                if i:
                    pe.wait_ge(s_mxq, b * NT + i)
                three(pPQ[:], xt(i), w(3 * D, HM)).then_inc(s_pq, 1)

            def turn_bias(b, i):
                g, t = i // T, i % T
                if t == 2 and g + 1 < GB:
                    pe.wait_ge(s_xl, b * GB + g + 2)
                pe.wait_ge(s_cl, b * NT + i + 1)
                nc.tensor.transpose(pT[:, 0:P], CHL[:, i % 2].rearrange("p a c h -> p (a c h)").bitcast(F32),
                                    ident[:]).then_inc(s_cT, 1)

            def bias_k(b, i):
                g, t = i // T, i % T
                pe.wait_ge(s_ct, b * NT + i + 1)
                pe.wait_ge(s_mxk, b * NT + i + 1)
                nc.tensor.matmul(pPK[i % 2][:], CT[:, g % 2, t * P:(t + 1) * P], selK[:],
                                 start=False, stop=True, skip_group_check=True).then_inc(s_pkb, 1)

            def sum_kv(b, i):
                pe.wait_ge(s_ek, b * NT + i + 1)
                pe.wait_ge(s_vx, b * NT + i + 1)
                v = VX[:, i % 3].rearrange("p h k -> p (h k)")
                nc.tensor.matmul(pKV[:, 0:VW], delta[:], v, start=(i == 0), stop=False, skip_group_check=True)
                for c in range(CH):
                    w = HC * KE
                    m = nc.tensor.matmul(pKV[:, c * w:(c + 1) * w], PK[:, i % 2, c * P:(c + 1) * P],
                                         v[:, c * w:(c + 1) * w], start=False, stop=(i == NT - 1 and c == CH - 1),
                                         skip_group_check=True)
                m.then_inc(s_kv, 1)

            def features_q(b, g):
                xt = [v[:, g % 2, :] for v in (XTH, XTL)]
                for c in range(CH):
                    if g * CH + c >= 2:
                        pe.wait_ge(s_eq, b * GB * CH + g * CH + c - 1)
                    w = [v[:, 3 * D + c * P:3 * D + (c + 1) * P] for v in (WH, WL)]
                    three(pF[c % 2][:], w, xt, stop=False)
                    nc.tensor.matmul(pF[c % 2][:], selQ[:, c * P:(c + 1) * P], CT[:, g % 2, :],
                                     start=False, stop=True).then_inc(s_fm, 1)

            with pe.Fori(0, B) as b:
                pe.wait_ge(s_batch, b + 1)
                turn_xn(b, 0)
                for i in range(NT + 2):
                    if i == NT:
                        features_q(b, GB - 2)
                    if i < NT:
                        qkv_pk(b, i)
                    if 1 <= i <= NT:
                        turn_bias(b, i - 1)
                    if i < NT:
                        pq(b, i)
                    if 1 <= i <= NT:
                        bias_k(b, i - 1)
                    if i >= 2:
                        sum_kv(b, i - 2)
                    if i % T == 1 and i > 1 and i // T != GB - 1:
                        features_q(b, i // T - 1)
                    if i % T == 2 and i < NT - T:
                        turn_xn(b, i // T + 1)
                pe.wait_ge(s_kvall, b + 1)
                nc.tensor.matmul(pT[:, 0:VW], delta[:], KVB[:], start=True, stop=True).then_inc(s_ds, 1)
                pe.wait_ge(s_dsc, b + 1)
                pe.wait_ge(s_eq, (b + 1) * GB * CH)

                def stage(g, k):
                    n = b * GB + g
                    if k == 0:
                        if g:
                            pe.wait_ge(s_nb, 2 * n)
                        w = HC * KE
                        for t in range(T):
                            for c in range(CH):
                                a = (t % 2) * VW + c * w
                                m = nc.tensor.matmul(pF[t // 2][:, a:a + w], PQT[:, g, c, t * P:(t + 1) * P],
                                                     KVB[:, c * w:(c + 1) * w], start=True, stop=True)
                            if t % 2:
                                m.then_inc(s_num, 1)
                    if k == 2:
                        if g == 1:
                            pe.wait_ge(s_att, n)
                        if g >= 2:
                            pe.wait_ge(s_x1t, n - 1)
                        pe.wait_ge(s_at, 2 * n + 2)
                        turn(pT, lambda t: AT[:, t].rearrange("p h k -> p (h k)")).then_inc(s_aT, 1)
                    if k == 3:
                        if g:
                            pe.wait_ge(s_r1, n)
                        pe.wait_ge(s_att, n + 1)
                        for t in range(T):
                            m = nc.tensor.matmul(pPQ[:, t * P:(t + 1) * P], ATT[:, t * P:(t + 1) * P], wo_s[:],
                                                 start=True, stop=True)
                        m.then_inc(s_wo, 1)
                    if k == 5:
                        pe.wait_ge(s_no[1], n + 1)
                        if g + 1 < GB:
                            pe.wait_ge(s_att, n + 2)
                        else:
                            pe.wait_ge(s_x1t, n)
                        turn(pT, lambda t: N1[:, t * P:(t + 1) * P]).then_inc(s_nT, 1)
                    if k == 7:
                        pe.wait_ge(s_x1t, n + 1)
                        for c in range(FC):
                            if g * FC + c >= 2:
                                pe.wait_ge(s_ge, n * FC + c - 1)
                            nc.tensor.matmul(pPK[c % 2][:], w1_s[:, c * P:(c + 1) * P], X1T,
                                             start=True, stop=True).then_inc(s_up, 1)
                    if k == 8:
                        if g:
                            pe.wait_ge(s_r2, n)
                        pe.wait_ge(s_ge, (n + 1) * FC)
                        for t in range(T):
                            for c in range(FC):
                                m = nc.tensor.matmul(pQKV[:, t * P:(t + 1) * P], HT[:, c, t * P:(t + 1) * P],
                                                     w2_s[:, c, :], start=(c == 0), stop=(c == FC - 1))
                        m.then_inc(s_dn, 1)
                    if k == 15:
                        pe.wait_ge(s_no[4], n + 1)
                        if g:
                            pe.wait_ge(s_xfl, n)
                        turn(pKV, lambda t: PL[:, g, t, 0, 0:D]).then_inc(s_fT, 1)
                    if k == 16:
                        pe.wait_ge(s_xft, n + 1)
                        pe.wait_ge(*((s_lgc, n) if g else (s_r1, (b + 1) * GB)))
                        for t in range(T):
                            m = nc.tensor.matmul(pPQ[:, t * E:(t + 1) * E], XFT[:, t * P:(t + 1) * P], gwT_s[:],
                                                 start=True, stop=True)
                        m.then_inc(s_lg, 1)
                        pe.wait_ge(s_xfl, n + 1)
                        for c in range(EC):
                            pe.wait_ge(*((s_ss1, n * EC + c - 1) if g or c >= 2 else (s_ge, (b + 1) * GB * FC)))
                            three(pPK[c % 2][:], [v[:, 0, c * P:(c + 1) * P] for v in (E1H, E1L)],
                                  [row(XFH, n), row(XFL, n)]).then_inc(s_su, 1)
                    if k == 18:
                        pe.wait_ge(*((s_base, n) if g else (s_x1t, (b + 1) * GB)))
                        pe.wait_ge(s_ohs, n + 1)
                        r = pT[:, 64:64 + T * E]
                        nc.tensor.matmul(r, before[:], OHS[:].rearrange("p t e -> p (t e)"), start=True, stop=False,
                                         skip_group_check=True)
                        for t in range(T - 1):
                            nc.tensor.matmul(r[:, (t + 1) * E:].rearrange("p (t e) -> p t e", e=E), ones_b[:],
                                             OHS[:, t:t + 1, :].to_broadcast([P, T - 1 - t, E]),
                                             start=False, stop=(t == T - 2), skip_group_check=True)
                        for t in range(T):
                            m = nc.tensor.matmul(pT[:, 128:128 + E], ones_b[:], OHS[:, t, :], start=(t == 0),
                                                 stop=(t == T - 1), skip_group_check=True)
                        m.then_inc(s_rt, 1)
                        pe.wait_ge(*((s_sh, n) if g else (s_r2, (b + 1) * GB)))
                        pe.wait_ge(s_w2, 16)
                        pe.wait_ge(s_ss1, (n + 1) * EC)
                        for t in range(T):
                            for c in range(EC):
                                m = nc.tensor.matmul(pQKV[:, t * P:(t + 1) * P], HT[:, c, t * P:(t + 1) * P],
                                                     E2[:, 0, c, :], start=(c == 0), stop=(c == EC - 1))
                        m.then_inc(s_sd, 1)

                pipeline(stage)

            banks = [pF[0], pF[1], pPK[0], pPK[1]]
            pe.wait_ge(s_tab, 13)
            pe.wait_ge(s_el, E + 1)
            pe.wait_ge(s_slot, NG)
            pe.wait_ge(s_sh, NG)
            turned = [pT, pKV]
            outs = [pQKV, pPQ]

            def turn_block(j, q):
                k = j * UNROLL + q
                wait(pe, s_bl, k - 1)
                pe.wait_ge(s_bx[q], j * 16 + 16)
                for t in range(2):
                    m = nc.tensor.transpose(turned[q % 2][:, t * P:(t + 1) * P], XS[q][:, t, 0:D], ident[:])
                m.then_inc(s_bT, 1)

            def weights_of(j, q):
                return pe.value_load(EW[0:1, bass.ds(j * UNROLL + q, 1)], min_val=0, max_val=E)

            def up_block(j, q, ew):
                for c in range(EC):
                    o = banks[q % 2 * 2 + c // 2][:, c % 2 * BW:(c % 2 + 1) * BW]
                    w = [v[:, bass.ds(ew, 1), c * P:(c + 1) * P].rearrange("p e h -> p (e h)") for v in (E1H, E1L)]
                    m = three(o, w, [XBH[:, q % 2, :], XBL[:, q % 2, :]])
                    if c % 2:
                        m.then_inc(s_u, 1)

            def down_block(j, q, ew):
                k = j * UNROLL + q
                wait(pe, s_y, k - 1)
                pe.wait_ge(s_si, 2 * k + 2)
                h = HT[:, q % 2 * 2:q % 2 * 2 + 2, :].rearrange("p a (c s) -> p (a c) s", s=BW)
                for t in range(2):
                    for c in range(EC):
                        w = E2[:, bass.ds(ew, 1), c, :].rearrange("p e d -> p (e d)")
                        m = nc.tensor.matmul(outs[q % 2][:, t * P:(t + 1) * P], h[:, c, t * P:(t + 1) * P], w,
                                             start=(c == 0), stop=(c == EC - 1))
                m.then_inc(s_do, 1)

            def blocks(j, last):
                for q in range(UNROLL):
                    k = j * UNROLL + q
                    wait(pe, s_si, 2 * k - 2)
                    pe.wait_ge(s_bl, k + 1)
                    if q + 1 < UNROLL:
                        turn_block(j, q + 1)
                    elif not last:
                        turn_block(j + 1, 0)
                    else:
                        nc.tensor.transpose(turned[(q + 1) % 2][:, 0:P], XS[q][:, 0, 0:D], ident[:])
                    up_block(j, q, weights_of(j, q))
                    if q:
                        down_block(j, q - 1, weights_of(j, q - 1))
                    elif not isinstance(j, int) or j:
                        down_block(j - 1, UNROLL - 1, weights_of(j - 1, UNROLL - 1))

            turn_block(0, 0)
            blocks(0, False)
            with pe.Fori(1, NBLK // UNROLL - 1) as j:
                blocks(j, False)
            j = NBLK // UNROLL - 1
            blocks(j, True)
            down_block(j, UNROLL - 1, weights_of(j, UNROLL - 1))

        @block.scalar
        def _(act):
            A = nc.scalar.activation

            def squares(b, i):
                act.wait_ge(s_qkv, b * NT + i + 1)
                if i >= 2:
                    act.wait_ge(s_ss, b * NT + i - 1)
                A(SQ[:, i % 2, :], pQKV[:, 0:2 * D], ACT.Square, scale=SCALE * 0.5 ** 0.5).then_inc(s_sq, 1)
                if i >= 3:
                    act.wait_ge(s_kv, b * NT + i - 2)
                A(VX[:, i % 3, :, 0:K], pQKV[:, 2 * D:3 * D].rearrange("p (h k) -> p h k", k=K),
                  ACT.Copy).then_inc(s_vx, 1)

            def exp_k(b, i):
                g, t = i // T, i % T
                act.wait_ge(s_cT, b * NT + i + 1)
                A(CT[:, g % 2, t * P:(t + 1) * P], pT[0:64, 0:P], ACT.Copy).then_inc(s_ct, 1)
                act.wait_ge(s_pkb, b * NT + i + 1)
                if i >= 2:
                    act.wait_ge(s_kv, b * NT + i - 1)
                A(PK[:, i % 2, :], pPK[i % 2][:], ACT.Exp).then_inc(s_ek, 1)

            def exp_q(b, g):
                for c in range(CH):
                    act.wait_ge(s_fm, (b * GB + g) * CH + c + 1)
                    A(PQT[:, g, c, :], pF[c % 2][:], ACT.Exp).then_inc(s_eq, 1)

            def hi_xn(b, g):
                act.wait_ge(s_xT, b * GB + g + 1)
                A(XTH[:, g % 2, :], pT[:], ACT.Copy).then_inc(s_xh, 1)

            act.wait_ge(s_ew1, 16)
            A(E1H[:].rearrange("p e h -> p (e h)").bitcast(BF16), EW1, ACT.Square, accum_out=ssum[:]).then_inc(s_ssq, 1)
            act.wait_ge(s_const, NCONST)
            act.wait_ge(s_sc, 3)
            with act.Fori(0, B) as b:
                act.wait_ge(s_batch, b + 1)
                hi_xn(b, 0)
                for i in range(NT + 2):
                    if i < NT:
                        squares(b, i)
                    if i == NT:
                        exp_q(b, GB - 2)
                    if 1 <= i <= NT:
                        exp_k(b, i - 1)
                    if i % T == 1 and i > 1 and i // T != GB - 1:
                        exp_q(b, i // T - 1)
                    if i % T == 2 and i < NT - T:
                        hi_xn(b, i // T + 1)

                def stage(g, k):
                    n = b * GB + g
                    if k == 2:
                        if g:
                            act.wait_ge(s_wo, n)
                        act.wait_ge(s_aT, n + 1)
                        A(ATT, pT[:], ACT.Copy).then_inc(s_att, 1)
                    if k == 14:
                        act.wait_ge(s_no[4], n + 1)
                        A(PL[:, g, :, 1, 0:D], PL[:, g, :, 0, 0:D], ACT.Copy).then_inc(s_cpy, 1)
                    if k == 6:
                        if g:
                            act.wait_ge(s_up, n * FC)
                        act.wait_ge(s_nT, n + 1)
                        A(X1T, pT[:], ACT.Identity, scale=cols_s[:, 0:1], bias=cols_s[:, 1:2]).then_inc(s_x1t, 1)
                    if k == 7:
                        if g:
                            act.wait_ge(s_dn, n)
                        for c in range(FC):
                            act.wait_ge(s_up, n * FC + c + 1)
                            A(HT[:, c, :], pPK[c % 2][:], ACT.Gelu, bias=cols_s[:, 2 + c:3 + c]).then_inc(s_ge, 1)
                    if k == 15:
                        if g:
                            act.wait_ge(s_lg, n)
                        act.wait_ge(s_fT, n + 1)
                        A(XFT, pKV[:], ACT.Copy).then_inc(s_xft, 1)
                        A(XFH[:, bass.ds(n, 1), :].rearrange("p n f -> p (n f)"), pKV[:], ACT.Copy).then_inc(s_xfh, 1)
                    if k == 16:
                        if g:
                            act.wait_ge(s_sd, n)
                        for c in range(EC):
                            act.wait_ge(s_su, n * EC + c + 1)
                            A(HT[:, c, :], pPK[c % 2][:], ACT.Silu, scale=wunscale[:]).then_inc(s_ss1, 1)
                    if k == 19:
                        act.wait_ge(s_sd, n + 1)
                        if g >= 2:
                            act.wait_ge(s_shst[g % 2], b * (16 * GB // 2) + 16 * (g // 2))
                        A(SH[g % 2], pQKV[:], ACT.Copy).then_inc(s_sh, 1)
                    if k == 17:
                        act.wait_ge(s_gd, n + 1)
                        A(TH[:], GA[:], ACT.Tanh, scale=0.5).then_inc(s_th, 1)

                pipeline(stage)
                for q in range(2):
                    act.wait_ge(s_shst[q], b * (16 * GB // 2) + 16 * GB // 2)

            banks = [pF[0], pF[1], pPK[0], pPK[1]]

            def hi_block(j, q):
                k = j * UNROLL + q
                wait(act, s_u, 2 * k - 2)
                act.wait_ge(s_bT, k + 1)
                A(XBH[:, q % 2, :], (pT, pKV)[q % 2][:, 0:BW], ACT.Copy).then_inc(s_bh, 1)

            def blocks(j, last):
                for q in range(UNROLL):
                    k = j * UNROLL + q
                    if q + 1 < UNROLL:
                        hi_block(j, q + 1)
                    elif not last:
                        hi_block(j + 1, 0)
                    for h in range(2):
                        if h == 0:
                            wait(act, s_do, k - 1)
                        act.wait_ge(s_u, 2 * k + h + 1)
                        A(HT[:, q % 2 * 2 + h, :], banks[q % 2 * 2 + h][:], ACT.Silu, scale=wunscale[:]).then_inc(s_si, 1)

            hi_block(0, 0)
            blocks(0, False)
            with act.Fori(1, NBLK // UNROLL - 1) as j:
                blocks(j, False)
            blocks(NBLK // UNROLL - 1, True)

            def norm_sum(i, q):
                n = i * 2 + q
                wait(act, s_out, n - 1)
                act.wait_ge(s_nm5, n + 1)
                for t in range(T):
                    s = A(N5[q][:, t * D:(t + 1) * D], ACC[q][:, t * D:(t + 1) * D], ACT.Identity,
                          scale=rs5[:, q, t:t + 1], bias=nm5[:, q, t:t + 1])
                s.then_inc(s_no5, 1)

            def store(i, q):
                act.wait_ge(s_out, i * 2 + q + 1)
                act.dma_start(out_v[bass.ds(i * 2 + q, 1)].rearrange("n p f -> (n p) f"), OUT[q]).then_inc(s_st[q], 16)

            norm_sum(0, 0)
            norm_sum(0, 1)
            store(0, 0)
            with act.Fori(1, NG // 2) as i:
                norm_sum(i, 0)
                store(i - 1, 1)
                norm_sum(i, 1)
                store(i, 0)
            store(NG // 2 - 1, 1)
            for q in range(2):
                act.wait_ge(s_st[q], 16 * (NG // 2))

        @block.vector
        def _(dve):
            v = nc.vector
            prep = [0]

            def prepared(ins):
                prep[0] += 1
                ins.then_inc(s_prep_v, 1)

            dve.wait_ge(s_w, 16 * NLOADS)
            dve.wait_ge(s_const, NCONST)
            prepared(v.tensor_tensor(omBD, omT_s.unsqueeze(1).to_broadcast([P, H, M]),
                                     headmask[:].unsqueeze(2).to_broadcast([P, H, M]), ALU.mult))
            dve.wait_ge(s_prep_v, 1)
            prepared(v.tensor_scalar(omBD_f, omBD_f, SCALE, None, ALU.mult))
            prepared(v.tensor_copy(WH[:, 0:3 * D], W_f))
            prepared(v.tensor_copy(selQ[:], sel_b[0:64]))
            prepared(v.tensor_copy(selK[:], MID[0:64, 0, :]))
            dve.wait_ge(s_prep_v, 3)
            prepared(v.tensor_tensor(WL[:, 0:3 * D], W_f, WH[:, 0:3 * D].bitcast(F32), ALU.subtract))
            for i in range(2):
                a = slice(3 * D + i * HM, 3 * D + (i + 1) * HM)
                dve.wait_ge(s_prep_p, i + 1)
                prepared(v.tensor_copy(WH[:, a], pF[i][:]))
                dve.wait_ge(s_prep_v, prep[0])
                prepared(v.tensor_tensor(WL[:, a], pF[i][:], WH[:, a].bitcast(F32), ALU.subtract))
            prepared(v.memset(CHL[:, :, 2:4].bitcast(F32), 0.0))
            prepared(v.tensor_copy(BASE[:], ecap[:]))
            prepared(v.memset(held[:], 0.0))
            dve.wait_ge(s_ssq, 2)
            v.tensor_scalar(hexp[:], stot[:].bitcast(U32), 24, None, ALU.logical_shift_right).then_inc(s_sc, 1)
            dve.wait_ge(s_sc, 1)
            v.tensor_scalar(wscale[:].bitcast(U32), hexp[:], -float(2 ** 23), 204.0 * 2 ** 23,
                            ALU.mult, ALU.add).then_inc(s_sc, 1)
            v.tensor_scalar(wunscale[:].bitcast(U32), hexp[:], float(2 ** 23), 50.0 * 2 ** 23,
                            ALU.mult, ALU.add).then_inc(s_sc, 1)
            dve.wait_ge(s_sc, 3)

            def split(e, at):
                hi, lo = row(E1H, e), row(E1L, e)
                v.tensor_scalar(hi, at, wscale[:], None, ALU.mult).then_inc(s_eh, 1)
                dve.wait_ge(s_eh, e + 1)
                v.scalar_tensor_tensor(out=lo, in0=at, scalar=wscale[:], in1=hi, op0=ALU.mult,
                                       op1=ALU.subtract).then_inc(s_el, 1)

            split(0, EW1[:, 0:HID])
            assert prep[0] == NPREP, prep
            dve.wait_ge(s_prep_v, prep[0])

            def hold(s, value, at=0):
                dve.wait_ge(s, value)
                v.memset(held[:, at:at + 1], 0.0)

            def stats(b, j, g, src):
                for t in range(T):
                    s = v.bn_stats(st[:, j, g, t, :], src[:, t * D:(t + 1) * D])
                s.then_inc(s_bn[j], 1)
                hold(s_bn[j], b * GB + g + 1)
                for t in range(T):
                    s = v.bn_aggr(mv[:, j, g, t, :], st[:, j, g, t, :])
                s.then_inc(s_mv[j], 1)

            def norm(b, j, g, dst, src):
                dve.wait_ge(s_rs[j], b * GB + g + 1)
                for t in range(T):
                    s = v.tensor_scalar(dst(t), src[:, t * D:(t + 1) * D],
                                        mv[:, j, g, t, 0:1], rs[:, j, g, t:t + 1], ALU.subtract, ALU.mult)
                s.then_inc(s_no[j], 1)

            def lo_xn(b, g):
                dve.wait_ge(s_xh, b * GB + g + 1)
                v.tensor_tensor(XTL[:, g % 2, :], pT[:], XTH[:, g % 2, :].bitcast(F32),
                                ALU.subtract).then_inc(s_xl, 1)

            def bias_parts(b, i):
                k = b * NT + i + 1
                dve.wait_ge(s_pk, k)
                v.tensor_reduce(MX[:, i % 2, 1, :], pPK[i % 2][:].rearrange("p (h m) -> p h m", m=M), AX_X,
                                ALU.max).then_inc(s_mxk, 1)
                dve.wait_ge(s_pq, k)
                v.tensor_reduce(MX[:, i % 2, 0, :], pPQ[:].rearrange("p (h m) -> p h m", m=M), AX_X,
                                ALU.max).then_inc(s_mxq, 1)
                dve.wait_ge(s_sq, k)
                v.tensor_reduce(SS[:, i % 2], SQ[:, i % 2, :].rearrange("p (a h k) -> p a h k", a=2, k=K), AX_X,
                                ALU.add).then_inc(s_ss, 1)
                dve.wait_ge(s_ss, k)
                dve.wait_ge(s_mxq, k)
                v.tensor_tensor(CC[:, i % 2], MX[:, i % 2], SS[:, i % 2], ALU.add).then_inc(s_cc, 1)
                dve.wait_ge(s_cc, k)
                if i >= 2:
                    dve.wait_ge(s_cT, k - 2)
                v.tensor_copy(CHL[:, i % 2, 0:2, 0, :], CC[:, i % 2]).then_inc(s_ch, 1)
                dve.wait_ge(s_ch, k)
                v.tensor_tensor(CHL[:, i % 2, 0:2, 1, :], CC[:, i % 2], CHL[:, i % 2, 0:2, 0, :].bitcast(F32),
                                ALU.subtract).then_inc(s_cl, 1)

            v.memset(held[:, 0:1], 0.0).then_inc(s_batch, 1)
            with dve.Fori(0, B) as b:
                dve.wait_ge(s_batch, b + 1)
                dve.wait_ge(s_x[0], b * 16 + 16)
                stats(b, 0, 0, row(X, b * GB))
                norm(b, 0, 0, tiles(XN[:, 0]), row(X, b * GB))
                lo_xn(b, 0)
                for i in range(NT):
                    g = i // T
                    bias_parts(b, i)
                    if g + 1 < GB:
                        if i % T == 0:
                            dve.wait_ge(s_x[g + 1], b * 16 + 16)
                            stats(b, 0, g + 1, row(X, b * GB + g + 1))
                        if i % T == 1:
                            norm(b, 0, g + 1, tiles(XN[:, g + 1]), row(X, b * GB + g + 1))
                        if i % T == 2:
                            lo_xn(b, g + 1)
                    if i % T == 3:
                        m = i // T
                        dve.wait_ge(s_stage[m], b * 16 + 16)
                        hold(s_stage[m], b * 16 + 16, at=0)
                        split(b * (E // B) + m + 1, W1S[:, m, :])
                dve.wait_ge(s_kv, (b + 1) * NT)
                v.tensor_tensor(KVB[:].rearrange("p (c j k) -> p c j k", c=CH, j=HC),
                                pKV[:, 0:VW].rearrange("p (c j k) -> p c j k", c=CH, j=HC),
                                kvmask[:].unsqueeze(1).unsqueeze(3).to_broadcast([P, CH, HC, KE]),
                                ALU.mult).then_inc(s_kvall, 1)
                dve.wait_ge(s_ds, b + 1)
                v.tensor_copy(DS[:], pT[:, 0:VW]).then_inc(s_dsc, 1)
                dve.wait_ge(s_dsc, b + 1)

                def stage(g, k):
                    n = b * GB + g
                    if k == 5:
                        if g:
                            dve.wait_ge(s_nT, n)
                            dve.wait_ge(s_n1g, n)
                        norm(b, 1, g, tiles(N1), R1)
                    if k == 6:
                        dve.wait_ge(s_no[1], n + 1)
                        x2, n1 = (u.rearrange("p (t d) -> p t d", t=T) for u in (XN[:, g], N1))
                        v.tensor_tensor(x2, n1, rows_s[:, 0, :].unsqueeze(1).to_broadcast([P, T, D]),
                                        ALU.mult).then_inc(s_n1g, 1)
                        dve.wait_ge(s_n1g, n + 1)
                        v.tensor_tensor(x2, x2, b12[:].unsqueeze(1).to_broadcast([P, T, D]), ALU.add).then_inc(s_x2, 1)
                    if k == 10:
                        if g >= 2:
                            dve.wait_ge(s_x1, n - 1)
                        norm(b, 2, g, tiles(NY[g % 2]), R2)
                    if k == 12:
                        norm(b, 3, g, tiles(NY[g % 2]), NY[g % 2])
                    if k == 14:
                        dve.wait_ge(s_free, b + 1)
                        norm(b, 4, g, lambda t: PL[:, g, t, 0, 0:D], row(X, n))
                    if k == 1:
                        if g:
                            dve.wait_ge(s_aT, n)
                        for h in range(2):
                            m = 2 * n + h + 1
                            dve.wait_ge(s_num, m)
                            nb = NB[:, h].rearrange("p t h k -> p t (h k)")
                            v.tensor_tensor(nb, pF[h][:, 0:2 * VW].rearrange("p (t w) -> p t w", t=2),
                                            DS[:].unsqueeze(1).to_broadcast([P, 2, VW]), ALU.add).then_inc(s_nb, 1)
                            dve.wait_ge(s_nb, m)
                            v.reciprocal(RD[:, h], NB[:, h, :, :, K]).then_inc(s_rd, 1)
                            dve.wait_ge(s_rd, m)
                            v.tensor_tensor(AT[:, 2 * h:2 * h + 2], NB[:, h, :, :, 0:K],
                                            RD[:, h].unsqueeze(3).to_broadcast([P, 2, H, K]), ALU.mult).then_inc(s_at, 1)
                    if k == 4:
                        dve.wait_ge(s_spare, 16 * GB)
                        if g:
                            dve.wait_ge(s_no[1], n)
                        dve.wait_ge(s_wo, n + 1)
                        v.tensor_tensor(R1, pPQ[:], XN[:, g], ALU.add).then_inc(s_r1, 1)
                        hold(s_r1, n + 1)
                        stats(b, 1, g, R1)
                    if k == 9:
                        if g:
                            dve.wait_ge(s_no[2], n)
                        dve.wait_ge(s_x2, n + 1)
                        dve.wait_ge(s_dn, n + 1)
                        v.tensor_tensor(R2, pQKV[:], XN[:, g], ALU.add).then_inc(s_r2, 1)
                        hold(s_r2, n + 1)
                        stats(b, 2, g, R2)
                    if k == 11:
                        hold(s_y2, n + 1, at=3)
                        stats(b, 3, g, NY[g % 2])
                    if k == 13:
                        hold(s_x1, n + 1, at=4)
                        stats(b, 4, g, row(X, n))
                    if k == 16:
                        dve.wait_ge(s_xfh, n + 1)
                        v.tensor_tensor(row(XFL, n), pKV[:], row(XFH, n), ALU.subtract).then_inc(s_xfl, 1)
                    if k == 17:
                        dve.wait_ge(s_lg, n + 1)
                        v.tensor_copy(LG[:].rearrange("p t e -> p (t e)"), pPQ[:, 0:T * E]).then_inc(s_lgc, 1)
                        hold(s_lgc, n + 1)
                        for t in range(T):
                            s = v.max(V8[:, t, :], LG[:, t, :])
                        s.then_inc(s_v8, 1)
                        hold(s_v8, n + 1)
                        for t in range(T):
                            s = v.max_index(I8[:, t, :], V8[:, t, :], LG[:, t, :])
                        s.then_inc(s_i8, 1)
                        v.tensor_tensor(GA[:], V8[:, :, 0], V8[:, :, 1], ALU.subtract).then_inc(s_gd, 1)
                        dve.wait_ge(s_i8, n + 1)
                        v.tensor_copy(I8f[:], I8[:, :, 0:TOPK]).then_inc(s_if, 1)
                        dve.wait_ge(s_if, n + 1)
                        for a in range(TOPK):
                            v.tensor_tensor(OH[:, a], iota8[:].unsqueeze(1).to_broadcast([P, T, E]),
                                            I8f[:, :, a:a + 1].to_broadcast([P, T, E]), ALU.is_equal).then_inc(s_oh, 1)
                        dve.wait_ge(s_oh, 2 * n + 2)
                        v.tensor_tensor(OHS[:], OH[:, 0], OH[:, 1], ALU.add).then_inc(s_ohs, 1)
                        v.tensor_copy(PL[:, g, :, :, ID_AT].bitcast(U32), IDS[:]).then_inc(s_pid, 1)
                        dve.wait_ge(s_pid, n + 1)
                        v.tensor_scalar(IDS[:], IDS[:], float(TOPK * GW), None, ALU.add).then_inc(s_ids, 1)
                        dve.wait_ge(s_ids, n + 1)
                    if k == 18:
                        dve.wait_ge(s_th, n + 1)
                        for a, sign in ((0, 0.5), (1, -0.5)):
                            v.tensor_scalar(PL[:, g, :, a, GATE_AT], TH[:], sign, 0.5, ALU.mult, ALU.add).then_inc(s_gt, 1)
                    if k == 19:
                        dve.wait_ge(s_rt, n + 1)
                        v.tensor_tensor(POS[:], pT[:, 64:64 + T * E].rearrange("p (t e) -> p t e", e=E),
                                        BASE[:].unsqueeze(1).to_broadcast([P, T, E]), ALU.add).then_inc(s_pos, 1)
                        dve.wait_ge(s_pos, n + 1)
                        v.tensor_tensor(BASE[:], pT[:, 128:128 + E], BASE[:], ALU.add).then_inc(s_base, 1)
                        v.tensor_tensor(OHP[:], OH[:], POS[:].unsqueeze(1).to_broadcast([P, TOPK, T, E]),
                                        ALU.mult).then_inc(s_ohp, 1)
                        dve.wait_ge(s_ohp, n + 1)
                        v.tensor_reduce(SLf[:].rearrange("p t a -> p a t"), OHP[:], AX_X, ALU.add).then_inc(s_slf, 1)
                        dve.wait_ge(s_slf, n + 1)
                        dve.wait_ge(s_gt, 2 * n + 2)
                        dve.wait_ge(s_base, n + 1)
                        v.tensor_copy(SLOT[:, g], SLf[:]).then_inc(s_slot, 1)

                pipeline(stage)
                dve.wait_ge(s_slot, (b + 1) * GB)
                dve.wait_ge(s_cpy, (b + 1) * GB)
                dve.wait_ge(s_sh, (b + 1) * GB)
                v.memset(held[:, 0:1], 0.0).then_inc(s_batch, 1)

            steps = [0]

            def step(ins):
                steps[0] += 1
                ins.then_inc(s_tab, 1)

            def settled():
                dve.wait_ge(s_tab, steps[0])

            step(v.tensor_copy(filslot[:], BASE[:]))
            step(v.tensor_tensor(CNT[:], BASE[:], ecap[:], ALU.subtract))
            settled()
            step(v.tensor_tensor(GTK, CNT[:].unsqueeze(2).to_broadcast([P, E, NK]),
                                 kb[:].unsqueeze(1).to_broadcast([P, E, NK]), ALU.is_gt))
            settled()
            step(v.tensor_reduce(NBK[:], GTK, AX_X, ALU.add))
            settled()
            step(v.tensor_tensor(CEM, leq[:], NBK[:].unsqueeze(1).to_broadcast([P, E, E]), ALU.mult))
            settled()
            step(v.tensor_reduce(CE[:], CEM, AX_X, ALU.add))
            settled()
            step(v.tensor_tensor(IND, jb[:].unsqueeze(2).to_broadcast([P, NBLK, E]),
                                 CE[:].unsqueeze(1).to_broadcast([P, NBLK, E]), ALU.is_ge))
            settled()
            step(v.tensor_reduce(EJ[:], IND, AX_X, ALU.add))
            step(v.tensor_tensor(INB, IND, NBK[:].unsqueeze(1).to_broadcast([P, NBLK, E]), ALU.mult))
            settled()
            step(v.tensor_reduce(CSJ[:], INB, AX_X, ALU.add))
            settled()
            v.tensor_tensor(RO[:], jb[:], CSJ[:], ALU.subtract).then_inc(s_pid, 1)
            dve.wait_ge(s_pid, NG + 1)
            v.tensor_scalar(ROWf[:], RO[:], float(BW), None, ALU.mult).then_inc(s_pid, 1)
            dve.wait_ge(s_pid, NG + 2)
            step(v.scalar_tensor_tensor(out=RO[:], in0=EJ[:], scalar=float(CAP), in1=ROWf[:], op0=ALU.mult, op1=ALU.add))
            settled()
            step(v.tensor_copy(ROW[:], RO[:]))
            step(v.tensor_scalar(EW[:], EJ[:], float(E - 1), 1.0, ALU.min, ALU.add))
            assert steps[0] == 13, steps

            def lo_block(j, q):
                k = j * UNROLL + q
                dve.wait_ge(s_bh, k + 1)
                v.tensor_tensor(XBL[:, q % 2, :], (pT, pKV)[q % 2][:, 0:BW], XBH[:, q % 2, :],
                                ALU.subtract).then_inc(s_bl, 1)

            def result(j, q):
                wait(dve, s_ysc[q], j * 32)
                dve.wait_ge(s_do, j * UNROLL + q + 1)
                for t in range(2):
                    s = v.tensor_scalar(Y[q][:, t, :], (pQKV, pPQ)[q % 2][:, t * P:(t + 1) * P],
                                        XS[q][:, t, GATE_AT:GATE_AT + 1], None, ALU.mult)
                s.then_inc(s_y, 1)

            def blocks(j, last):
                for q in range(UNROLL):
                    if q + 1 < UNROLL:
                        lo_block(j, q + 1)
                    elif not last:
                        lo_block(j + 1, 0)
                    if q:
                        result(j, q - 1)
                    elif not isinstance(j, int) or j:
                        result(j - 1, UNROLL - 1)

            lo_block(0, 0)
            blocks(0, False)
            with dve.Fori(1, NBLK // UNROLL - 1) as j:
                blocks(j, False)
            blocks(NBLK // UNROLL - 1, True)
            result(NBLK // UNROLL - 1, UNROLL - 1)

            def sum_stats(i, q):
                n = i * 2 + q
                dve.wait_ge(s_ya, n + 1)
                dve.wait_ge(s_shst[q], i * 16 + (NG // 2 + 1) * 16)
                wait(dve, s_no5, n - 1)
                v.tensor_tensor(ACC[q], SH[q], AY[q], ALU.add).then_inc(s_acc, 1)
                hold(s_acc, n + 1)
                for t in range(T):
                    s = v.bn_stats(st5[:, q, t, :], ACC[q][:, t * D:(t + 1) * D])
                s.then_inc(s_bn5, 1)
                hold(s_bn5, n + 1)
                for t in range(T):
                    s = v.bn_aggr(mv5[:, q, t, :], st5[:, q, t, :])
                s.then_inc(s_mv5, 1)

            def residual(i, q):
                n = i * 2 + q
                wait(dve, s_st[q], i * 16)
                dve.wait_ge(s_no5, n + 1)
                v.tensor_tensor(OUT[q], row(X, n), N5[q], ALU.add).then_inc(s_out, 1)

            sum_stats(0, 0)
            with dve.Fori(0, NG // 2 - 1) as i:
                sum_stats(i, 1)
                residual(i, 0)
                sum_stats(i + 1, 0)
                residual(i, 1)
            sum_stats(NG // 2 - 1, 1)
            residual(NG // 2 - 1, 0)
            residual(NG // 2 - 1, 1)


_OUTS = [((B, S, D), 'float32')]


def kernel(**inputs):
    import numpy as np
    import concourse.bacc as bacc
    from concourse import mybir as mb
    from concourse.bass_utils import run_bass_kernel_spmd as run

    f = lambda n: np.asarray(inputs[n])
    wq, wk, wv = (f(f"L0_attn_{n}").reshape(D, H * K) for n in ("wq", "wk", "wv"))
    arrays = {
        "x": f("L0_attn_x"),
        "wqkv": np.concatenate([wq, wk, wv], axis=1),
        "wqkT": np.stack([wq.T, wk.T], axis=1),
        "omT": np.tile(f("L0_attn_omega").T, (H, 1)),
        "wo": f("L0_attn_wo"),
        "cols": np.concatenate([f("L0_attn_ln1_g")[:, None], f("L0_attn_ln1_b")[:, None],
                                f("L0_attn_b1").reshape(FC, P).T], axis=1),
        "rows": np.concatenate([f(f"L0_attn_{n}") for n in ("ln1_g", "ln1_b", "b2", "ln2_g", "ln2_b")])[None, :],
        "w1": f("L0_attn_w1"),
        "w2": f("L0_attn_w2").reshape(FC, P, D).transpose(1, 0, 2),
        "ew1T": np.concatenate([f("L0_ffn_shared_w1")[None], f("L0_ffn_experts_w1")]).transpose(2, 0, 1),
        "ew2T": np.concatenate([f("L0_ffn_shared_w2")[None], f("L0_ffn_experts_w2")])
                  .reshape(E + 1, D, EC, P).transpose(3, 0, 2, 1),
        "gwT": f("L0_ffn_gate_w").T,
    }
    nc = bacc.Bacc("TRN2", target_bir_lowering=False, num_devices=1)
    feed, args = {}, []
    for name, a in arrays.items():
        a = np.ascontiguousarray(a)
        feed[f"in_{name}"] = a
        args.append(nc.dram_tensor(f"in_{name}", a.shape, mb.dt.from_np(a.dtype), kind="ExternalInput").ap())
    for i, (shape, dtype) in enumerate(_OUTS):
        args.append(nc.dram_tensor(f"out_{i}", shape, mb.dt.from_np(np.dtype(dtype)), kind="ExternalOutput").ap())
    xs = nc.dram_tensor("xs", (XROWS, RW), mb.dt.float32).ap()
    ys = nc.dram_tensor("ys", (YROWS, D), mb.dt.float32).ap()
    sh = nc.dram_tensor("sh", (NG, P, GW), mb.dt.float32).ap()
    build(nc, xs, ys, sh, *args)
    r = run(nc, [feed], core_ids=[0])
    return r.results[0]["out_0"]
```
